# Optimizing a Trainium2 kernel written in Bass

```python
import numpy as np
import jax
import jax.numpy as jnp

def _softmax(x, axis=-1):
    return jax.nn.softmax(x, axis=axis)

def _gelu(x):
    return jax.nn.gelu(x, approximate=True)

def _silu(x):
    return jax.nn.silu(x)

def _sigmoid(x):
    return jax.nn.sigmoid(x)

def _layernorm(x, axis=-1, eps=1e-05):
    m = jnp.mean(x, axis=axis, keepdims=True)
    v = jnp.var(x, axis=axis, keepdims=True)
    return (x - m) / jnp.sqrt(v + eps)

def _scatter_add(tgt, idx, src, axis=0):
    return tgt.at[idx].add(src)

def _segment_sum(src, seg, n):
    return jax.ops.segment_sum(src, seg, n)
kernel_name = 'mk_hybrid_d1_jaxref_r8_60295c'

def setup_inputs(seed: int=0):
    np.random.seed(seed)
    _w = jnp.asarray

    def _L0_attn_a_setup():
        import jax, jax.numpy as jnp
        import numpy as np
        MODEL_DIM = 128
        NUM_HEADS = 16
        HEAD_DIM = MODEL_DIM // NUM_HEADS
        EPS = 1e-12
        CHUNK = 128

        def _pos_elu(t):
            return jax.nn.elu(t) + 1.0

        def _linear_attention(q, k, v):
            b, h, l, d = q.shape
            nc = l // CHUNK
            qc = jnp.moveaxis(q.reshape(b, h, nc, CHUNK, d), 2, 0)
            kc = jnp.moveaxis(k.reshape(b, h, nc, CHUNK, d), 2, 0)
            vc = jnp.moveaxis(v.reshape(b, h, nc, CHUNK, d), 2, 0)
            mask = jnp.tril(jnp.ones((CHUNK, CHUNK), dtype=q.dtype))

            def step(carry, inp):
                S, z = carry
                qb, kb, vb = inp
                scores = jnp.einsum('bhcd,bhsd->bhcs', qb, kb) * mask
                num = jnp.einsum('bhcd,bhde->bhce', qb, S) + jnp.einsum('bhcs,bhse->bhce', scores, vb)
                den = jnp.einsum('bhcd,bhd->bhc', qb, z) + scores.sum(-1)
                out = num / den[..., None] + EPS
                S = S + jnp.einsum('bhsd,bhse->bhde', kb, vb)
                z = z + kb.sum(axis=2)
                return ((S, z), out)
            S0 = jnp.zeros((b, h, d, d), dtype=q.dtype)
            z0 = jnp.zeros((b, h, d), dtype=q.dtype)
            _, outs = jax.lax.scan(step, (S0, z0), (qc, kc, vc))
            return jnp.moveaxis(outs, 0, 1).transpose(0, 3, 1, 2, 4).reshape(b, h * 0 + l // l, 0, 0) if False else outs
        key = jax.random.key(seed)
        kx, kq, kk, kv, ko = jax.random.split(key, 5)
        b, l = (4, 512)
        x = jax.random.normal(kx, (b, l, MODEL_DIM), dtype=jnp.float32)
        Wq = 0.02 * jax.random.normal(kq, (MODEL_DIM, MODEL_DIM), dtype=jnp.float32)
        Wk = 0.02 * jax.random.normal(kk, (MODEL_DIM, MODEL_DIM), dtype=jnp.float32)
        Wv = 0.02 * jax.random.normal(kv, (MODEL_DIM, MODEL_DIM), dtype=jnp.float32)
        Wo = 0.02 * jax.random.normal(ko, (MODEL_DIM, MODEL_DIM), dtype=jnp.float32)
        return {'x': x, 'Wq': Wq, 'Wk': Wk, 'Wv': Wv, 'Wo': Wo}
    _L0_attn_a_in = _L0_attn_a_setup()

    def _L0_attn_b_setup():
        import jax, jax.numpy as jnp
        import numpy as np
        DIM = 128
        D_STATE = 16
        D_CONV = 4
        EXPAND = 2
        D_INNER = EXPAND * DIM
        B = 4
        L = 256

        def _forward(x, W_in, conv_w, conv_b, W_xproj, W_dt, b_dt, A_log, Dp, W_out):
            Bb, Ll, _ = x.shape
            xz = x @ W_in
            xc, z = jnp.split(xz, 2, axis=-1)
            xc = jnp.transpose(xc, (0, 2, 1))
            xc = jax.lax.conv_general_dilated(xc, conv_w, window_strides=(1,), padding=((D_CONV - 1, 0),), dimension_numbers=('NCH', 'OIH', 'NCH'), feature_group_count=D_INNER)
            xc = xc + conv_b[None, :, None]
            xc = jnp.transpose(xc, (0, 2, 1))
            xc = jax.nn.silu(xc)
            B_ssm = (xc @ W_xproj)[..., D_STATE:]
            delta = jax.nn.softplus(xc @ W_dt + b_dt)
            A = -jnp.exp(A_log)
            deltaA = jnp.exp(delta[..., None] * A)
            dx = delta * xc

            def step(s, t):
                dA_t, dx_t, B_t, x_t = t
                s = dA_t * s + dx_t[:, :, None] * B_t[:, None, :]
                y = jnp.einsum('bdn,bn->bd', s, B_t) + Dp * x_t
                return (s, y)
            s0 = jnp.zeros((Bb, D_INNER, D_STATE), x.dtype)
            _, ys = jax.lax.scan(step, s0, (jnp.transpose(deltaA, (1, 0, 2, 3)), jnp.transpose(dx, (1, 0, 2)), jnp.transpose(B_ssm, (1, 0, 2)), jnp.transpose(xc, (1, 0, 2))))
            y = jnp.transpose(ys, (1, 0, 2)) * jax.nn.silu(z)
            return y @ W_out
        key = jax.random.key(seed)
        ks = jax.random.split(key, 7)

        def rn(k, shape, scale):
            return jax.random.normal(k, shape, dtype=jnp.float32) * scale
        x = jax.random.normal(ks[0], (B, L, DIM), dtype=jnp.float32)
        W_in = rn(ks[1], (DIM, 2 * D_INNER), DIM ** (-0.5))
        conv_w = rn(ks[2], (D_INNER, 1, D_CONV), D_CONV ** (-0.5))
        conv_b = jnp.zeros((D_INNER,), jnp.float32)
        W_xproj = rn(ks[3], (D_INNER, 2 * D_STATE), D_INNER ** (-0.5))
        W_dt = rn(ks[4], (D_INNER, D_INNER), D_INNER ** (-0.5))
        b_dt = jnp.zeros((D_INNER,), jnp.float32)
        A_log = jnp.log(jnp.broadcast_to(jnp.arange(1, D_STATE + 1, dtype=jnp.float32), (D_INNER, D_STATE)))
        Dp = jnp.ones((D_INNER,), jnp.float32)
        W_out = rn(ks[5], (D_INNER, DIM), D_INNER ** (-0.5))
        return dict(x=x, W_in=W_in, conv_w=conv_w, conv_b=conv_b, W_xproj=W_xproj, W_dt=W_dt, b_dt=b_dt, A_log=A_log, Dp=Dp, W_out=W_out)
    _L0_attn_b_in = _L0_attn_b_setup()

    def _L0_ffn_setup():
        import jax, jax.numpy as jnp
        import numpy as np
        DIM = 128

        def _reference_tuple_inner(x, W_r, W_k, W_v, mu_r, mu_k):
            B, T, C = x.shape
            x_prev = jnp.concatenate([jnp.zeros((B, 1, C), x.dtype), x[:, :-1, :]], axis=1)
            xr = mu_r * x + (1.0 - mu_r) * x_prev
            xk = mu_k * x + (1.0 - mu_k) * x_prev
            r = jax.nn.sigmoid(jnp.einsum('btc,dc->btd', xr, W_r))
            k = jnp.einsum('btc,dc->btd', xk, W_k)
            k_act = jnp.square(jax.nn.relu(k))
            out = r * jnp.einsum('btc,dc->btd', k_act, W_v)
            new_state = x[:, -1, :]
            return (out, new_state)
        key = jax.random.key(seed)
        ks = jax.random.split(key, 6)
        B, T, C = (8, 256, DIM)
        x = jax.random.normal(ks[0], (B, T, C), dtype=jnp.float32)
        s = 1.0 / np.sqrt(C)
        W_r = jax.random.uniform(ks[1], (C, C), jnp.float32, -s, s)
        W_k = jax.random.uniform(ks[2], (C, C), jnp.float32, -s, s)
        W_v = jax.random.uniform(ks[3], (C, C), jnp.float32, -s, s)
        mu_r = jax.random.uniform(ks[4], (C,), jnp.float32)
        mu_k = jax.random.uniform(ks[5], (C,), jnp.float32)
        return {'x': x, 'W_r': W_r, 'W_k': W_k, 'W_v': W_v, 'mu_r': mu_r, 'mu_k': mu_k}
    _L0_ffn_in = _L0_ffn_setup()
    _d = {'L0_attn_a_x': _L0_attn_a_in['x'], 'L0_attn_a_Wq': _L0_attn_a_in['Wq'], 'L0_attn_a_Wk': _L0_attn_a_in['Wk'], 'L0_attn_a_Wv': _L0_attn_a_in['Wv'], 'L0_attn_a_Wo': _L0_attn_a_in['Wo'], 'L0_attn_b_W_in': _L0_attn_b_in['W_in'], 'L0_attn_b_conv_w': _L0_attn_b_in['conv_w'], 'L0_attn_b_conv_b': _L0_attn_b_in['conv_b'], 'L0_attn_b_W_xproj': _L0_attn_b_in['W_xproj'], 'L0_attn_b_W_dt': _L0_attn_b_in['W_dt'], 'L0_attn_b_b_dt': _L0_attn_b_in['b_dt'], 'L0_attn_b_A_log': _L0_attn_b_in['A_log'], 'L0_attn_b_Dp': _L0_attn_b_in['Dp'], 'L0_attn_b_W_out': _L0_attn_b_in['W_out'], 'L0_ffn_W_r': _L0_ffn_in['W_r'], 'L0_ffn_W_k': _L0_ffn_in['W_k'], 'L0_ffn_W_v': _L0_ffn_in['W_v'], 'L0_ffn_mu_r': _L0_ffn_in['mu_r'], 'L0_ffn_mu_k': _L0_ffn_in['mu_k']}
    _x0 = _d['L0_attn_a_x']
    _d['L0_attn_a_x'] = jax.random.normal(jax.random.fold_in(jax.random.key(seed), 1), (32, 256, 128), dtype=_x0.dtype)
    del _x0
    return _d

def reference(L0_attn_a_x, L0_attn_a_Wq, L0_attn_a_Wk, L0_attn_a_Wv, L0_attn_a_Wo, L0_attn_b_W_in, L0_attn_b_conv_w, L0_attn_b_conv_b, L0_attn_b_W_xproj, L0_attn_b_W_dt, L0_attn_b_b_dt, L0_attn_b_A_log, L0_attn_b_Dp, L0_attn_b_W_out, L0_ffn_W_r, L0_ffn_W_k, L0_ffn_W_v, L0_ffn_mu_r, L0_ffn_mu_k):

    def _L0_attn_a_ref(x, Wq, Wk, Wv, Wo):
        import jax, jax.numpy as jnp
        import numpy as np
        MODEL_DIM = 128
        NUM_HEADS = 16
        HEAD_DIM = MODEL_DIM // NUM_HEADS
        EPS = 1e-12
        CHUNK = 128

        def _pos_elu(t):
            return jax.nn.elu(t) + 1.0

        def _linear_attention(q, k, v):
            b, h, l, d = q.shape
            nc = l // CHUNK
            qc = jnp.moveaxis(q.reshape(b, h, nc, CHUNK, d), 2, 0)
            kc = jnp.moveaxis(k.reshape(b, h, nc, CHUNK, d), 2, 0)
            vc = jnp.moveaxis(v.reshape(b, h, nc, CHUNK, d), 2, 0)
            mask = jnp.tril(jnp.ones((CHUNK, CHUNK), dtype=q.dtype))

            def step(carry, inp):
                S, z = carry
                qb, kb, vb = inp
                scores = jnp.einsum('bhcd,bhsd->bhcs', qb, kb) * mask
                num = jnp.einsum('bhcd,bhde->bhce', qb, S) + jnp.einsum('bhcs,bhse->bhce', scores, vb)
                den = jnp.einsum('bhcd,bhd->bhc', qb, z) + scores.sum(-1)
                out = num / den[..., None] + EPS
                S = S + jnp.einsum('bhsd,bhse->bhde', kb, vb)
                z = z + kb.sum(axis=2)
                return ((S, z), out)
            S0 = jnp.zeros((b, h, d, d), dtype=q.dtype)
            z0 = jnp.zeros((b, h, d), dtype=q.dtype)
            _, outs = jax.lax.scan(step, (S0, z0), (qc, kc, vc))
            return jnp.moveaxis(outs, 0, 1).transpose(0, 3, 1, 2, 4).reshape(b, h * 0 + l // l, 0, 0) if False else outs
        b, l, D = x.shape
        h, d = (NUM_HEADS, HEAD_DIM)
        q = (x @ Wq.T).reshape(b, l, h, d).transpose(0, 2, 1, 3)
        k = (x @ Wk.T).reshape(b, l, h, d).transpose(0, 2, 1, 3)
        v = (x @ Wv.T).reshape(b, l, h, d).transpose(0, 2, 1, 3)
        q = _pos_elu(q)
        k = _pos_elu(k)
        outs = _linear_attention(q, k, v)
        nc = l // CHUNK
        attn = outs.transpose(1, 0, 3, 2, 4).reshape(b, l, D)
        return attn @ Wo.T

    def _L0_attn_b_ref(x, W_in, conv_w, conv_b, W_xproj, W_dt, b_dt, A_log, Dp, W_out):
        import jax, jax.numpy as jnp
        import numpy as np
        DIM = 128
        D_STATE = 16
        D_CONV = 4
        EXPAND = 2
        D_INNER = EXPAND * DIM
        B = 4
        L = 256

        def _forward(x, W_in, conv_w, conv_b, W_xproj, W_dt, b_dt, A_log, Dp, W_out):
            Bb, Ll, _ = x.shape
            xz = x @ W_in
            xc, z = jnp.split(xz, 2, axis=-1)
            xc = jnp.transpose(xc, (0, 2, 1))
            xc = jax.lax.conv_general_dilated(xc, conv_w, window_strides=(1,), padding=((D_CONV - 1, 0),), dimension_numbers=('NCH', 'OIH', 'NCH'), feature_group_count=D_INNER)
            xc = xc + conv_b[None, :, None]
            xc = jnp.transpose(xc, (0, 2, 1))
            xc = jax.nn.silu(xc)
            B_ssm = (xc @ W_xproj)[..., D_STATE:]
            delta = jax.nn.softplus(xc @ W_dt + b_dt)
            A = -jnp.exp(A_log)
            deltaA = jnp.exp(delta[..., None] * A)
            dx = delta * xc

            def step(s, t):
                dA_t, dx_t, B_t, x_t = t
                s = dA_t * s + dx_t[:, :, None] * B_t[:, None, :]
                y = jnp.einsum('bdn,bn->bd', s, B_t) + Dp * x_t
                return (s, y)
            s0 = jnp.zeros((Bb, D_INNER, D_STATE), x.dtype)
            _, ys = jax.lax.scan(step, s0, (jnp.transpose(deltaA, (1, 0, 2, 3)), jnp.transpose(dx, (1, 0, 2)), jnp.transpose(B_ssm, (1, 0, 2)), jnp.transpose(xc, (1, 0, 2))))
            y = jnp.transpose(ys, (1, 0, 2)) * jax.nn.silu(z)
            return y @ W_out
        return _forward(x, W_in, conv_w, conv_b, W_xproj, W_dt, b_dt, A_log, Dp, W_out)

    def _L0_ffn_ref(x, W_r, W_k, W_v, mu_r, mu_k):
        import jax, jax.numpy as jnp
        import numpy as np
        DIM = 128

        def _reference_tuple_inner(x, W_r, W_k, W_v, mu_r, mu_k):
            B, T, C = x.shape
            x_prev = jnp.concatenate([jnp.zeros((B, 1, C), x.dtype), x[:, :-1, :]], axis=1)
            xr = mu_r * x + (1.0 - mu_r) * x_prev
            xk = mu_k * x + (1.0 - mu_k) * x_prev
            r = jax.nn.sigmoid(jnp.einsum('btc,dc->btd', xr, W_r))
            k = jnp.einsum('btc,dc->btd', xk, W_k)
            k_act = jnp.square(jax.nn.relu(k))
            out = r * jnp.einsum('btc,dc->btd', k_act, W_v)
            new_state = x[:, -1, :]
            return (out, new_state)
        return _reference_tuple_inner(x, W_r, W_k, W_v, mu_r, mu_k)[0]
    x = L0_attn_a_x
    x = x + _L0_attn_a_ref(_layernorm(x, axis=-1), L0_attn_a_Wq, L0_attn_a_Wk, L0_attn_a_Wv, L0_attn_a_Wo)
    x = x + _L0_ffn_ref(_layernorm(x, axis=-1), L0_ffn_W_r, L0_ffn_W_k, L0_ffn_W_v, L0_ffn_mu_r, L0_ffn_mu_k)
    x = x + _L0_attn_b_ref(_layernorm(x, axis=-1), L0_attn_b_W_in, L0_attn_b_conv_w, L0_attn_b_conv_b, L0_attn_b_W_xproj, L0_attn_b_W_dt, L0_attn_b_b_dt, L0_attn_b_A_log, L0_attn_b_Dp, L0_attn_b_W_out)
    x = x + _L0_ffn_ref(_layernorm(x, axis=-1), L0_ffn_W_r, L0_ffn_W_k, L0_ffn_W_v, L0_ffn_mu_r, L0_ffn_mu_k)
    return x

_drawn_inputs = setup_inputs


def setup_inputs(seed=0):
    import zlib

    import numpy as np

    out = dict(_drawn_inputs(seed))
    spreads = {'L0_attn_b_conv_b': (0.0, 0.1), 'L0_attn_b_b_dt': (0.0, 0.1), 'L0_attn_b_Dp': (1.0, 0.2)}
    factors = {'L0_attn_a_Wq': 8.0,
     'L0_attn_a_Wk': 8.0,
     'L0_attn_a_Wv': 5.022,
     'L0_attn_a_Wo': 5.077,
     'L0_ffn_mu_r': 4.016}
    for name, (base, spread) in spreads.items():
        noise = np.random.default_rng([zlib.crc32(name.encode()), seed]).standard_normal(out[name].shape)
        drawn = base * np.exp(spread * noise) if base else spread * noise
        out[name] = jnp.asarray(drawn.astype(out[name].dtype))
    for name, factor in factors.items():
        out[name] = (out[name] * factor).astype(out[name].dtype)
    return out
```

```python
from contextlib import ExitStack

import concourse.bass as bass
from concourse import mybir

P = 128
SEQ = 256
NSEQ = 32
SU = 2
UC = SU * SEQ
TU = UC // P
NU = NSEQ // SU
H, HD = 16, 8
HE = HD + 1
DI = 2
NS = 16
TAPS = 4
LN_EPS, ATT_EPS = 1e-5, 1e-12

F32, BF16 = mybir.dt.float32, mybir.dt.bfloat16
ALU = mybir.AluOpType
ACT = mybir.ActivationFunctionType
AX_X = mybir.AxisListType.X
LAYERS = ("att", "ffn1", "mamba", "ffn2")
EXP_LN_SET = 6


def over_units(eng, body):
    body(0, 0, True, False)
    body(1, 1, False, False)
    with eng.Fori(0, (NU - 4) // 2) as i:
        body(i * 2 + 2, 0, False, False)
        body(i * 2 + 3, 1, False, False)
    body(NU - 2, 0, False, False)
    body(NU - 1, 1, False, True)


def is_unit(u):
    return not isinstance(u, int) or u < NU


def after(eng, sem, count):
    if not isinstance(count, int) or count > 0:
        eng.wait_ge(sem, count)


class Memory:

    def __init__(self, nc, ctx, layer):
        self.nc, self.ctx, self.layer = nc, ctx, layer

    def sb(self, name, shape, dtype=F32):
        return self.ctx.enter_context(self.nc.sbuf_tensor(f"{self.layer}_{name}", shape, dtype))

    def ps(self, name, shape, dtype=F32):
        return self.ctx.enter_context(self.nc.psum_tensor(f"{self.layer}_{name}", shape, dtype))

    def sem(self, name):
        return self.ctx.enter_context(self.nc.semaphore(f"{self.layer}_{name}"))


def unit_cols(x_res, u, c0=0, c1=UC):
    return x_res[:, bass.ds(u, 1), c0:c1].rearrange("p o c -> p (o c)")


class Front:

    def __init__(self, nc, m, x_res, ident, neg_half, eps):
        self.nc, self.x_res, self.ident, self.neg_half, self.eps = nc, x_res, ident, neg_half, eps
        self.stats = m.sb("stats", [P, TU, 6])
        self.mean_var = m.sb("mean_var", [P, TU, 2])
        self.var_eps = m.sb("var_eps", [P, TU])
        self.rstd = m.sb("rstd", [P, TU])
        self.pad = m.sb("pad", [P, 1])
        self.xn = m.sb("xn", [P, UC])
        self.ps_t = m.ps("ps_t", [P, UC])
        self.stats_ready = m.sem("stats_ready")
        self.mean_ready = m.sem("mean_ready")
        self.eps_ready = m.sem("eps_ready")
        self.rstd_ready = m.sem("rstd_ready")
        self.xn_ready = m.sem("xn_ready")
        self.xn_transposed = m.sem("xn_transposed")

    def vector_stats(self, dve, u):
        nc = self.nc
        for j in range(TU):
            op = nc.vector.bn_stats(self.stats[:, j, :], unit_cols(self.x_res, u, j * P, (j + 1) * P))
        op.then_inc(self.stats_ready, 1)
        dve.wait_ge(self.stats_ready, u + 1)
        nc.vector.memset(self.pad[:], 0.0)
        for j in range(TU):
            op = nc.vector.bn_aggr(self.mean_var[:, j, :], self.stats[:, j, :])
        op.then_inc(self.mean_ready, 1)

    def gpsimd_rstd(self, pool, u):
        nc = self.nc
        pool.wait_ge(self.mean_ready, u + 1)
        nc.gpsimd.tensor_tensor(self.var_eps[:], self.mean_var[:, :, 1], self.eps[:],
                                ALU.add).then_inc(self.eps_ready, 1)
        pool.wait_ge(self.eps_ready, u + 1)
        nc.gpsimd.tensor_tensor(self.rstd[:], self.var_eps[:], self.neg_half[:],
                                ALU.pow).then_inc(self.rstd_ready, 1)

    def vector_normalise(self, dve, u, first):
        nc = self.nc
        dve.wait_ge(self.rstd_ready, u + 1)
        if not first:
            dve.wait_ge(self.xn_transposed, u)
        for j in range(TU):
            op = nc.vector.tensor_scalar(self.xn[:, j * P:(j + 1) * P],
                                         unit_cols(self.x_res, u, j * P, (j + 1) * P),
                                         self.mean_var[:, j, 0:1], self.rstd[:, j:j + 1],
                                         ALU.subtract, ALU.mult)
        op.then_inc(self.xn_ready, 1)

    def tensor_transpose(self, pe, u):
        nc = self.nc
        pe.wait_ge(self.xn_ready, u + 1)
        for j in range(TU):
            op = nc.tensor.transpose(self.ps_t[:, j * P:(j + 1) * P], self.xn[:, j * P:(j + 1) * P],
                                     self.ident[:])
        op.then_inc(self.xn_transposed, 1)


def seqs(ap):
    return ap.rearrange("p (s t) -> p s t", s=SU)


def ffn_layer(nc, layer, x_res, ident, neg_half, eps, weights, out_dram):
    wr_dram, wk_dram, wv_dram, mu_r_dram, mu_k_dram = weights
    with ExitStack() as ctx:
        m = Memory(nc, ctx, layer)
        front = Front(nc, m, x_res, ident, neg_half, eps)
        wr, wk, wv = (m.sb(n, [P, P]) for n in ("wr", "wk", "wv"))
        mu_r, mu_k = m.sb("mu_r", [P, 1]), m.sb("mu_k", [P, 1])
        xt = m.sb("xt", [P, 2, SU, SEQ + 1])
        diff = m.sb("diff", [P, 2, UC])
        xr, xk = m.sb("xr", [P, UC]), m.sb("xk", [P, UC])
        tanh_r = m.sb("tanh_r", [P, 2, UC])
        relu_k = m.sb("relu_k", [P, UC])
        k_act = m.sb("k_act", [P, 2, UC])
        gated = m.sb("gated", [P, UC])
        ps_r, ps_k, ps_v = (m.ps(n, [P, UC]) for n in ("ps_r", "ps_k", "ps_v"))
        weights_loaded = m.sem("weights_loaded")
        zero_ready = m.sem("zero_ready")
        xt_ready = m.sem("xt_ready")
        diff_ready = m.sem("diff_ready")
        mix_ready = m.sem("mix_ready")
        k_ready = m.sem("k_ready")
        rk_ready = m.sem("rk_ready")
        tanh_ready = m.sem("tanh_ready")
        relu_ready = m.sem("relu_ready")
        k_act_ready = m.sem("k_act_ready")
        v_ready = m.sem("v_ready")
        gated_ready = m.sem("gated_ready")
        x_ready = m.sem("x_ready")
        stored = m.sem("stored")
        block = ctx.enter_context(nc.Block())

        @block.sync
        def _(sp):
            for dst, src in ((wr, wr_dram), (wk, wk_dram), (wv, wv_dram), (mu_r, mu_r_dram), (mu_k, mu_k_dram)):
                sp.dma_start(dst[:], src).then_inc(weights_loaded, 16)
            if out_dram is not None:
                with sp.Fori(0, NU) as u:
                    sp.wait_ge(x_ready, u + 1)
                    sp.dma_start(unit_cols(out_dram, u), unit_cols(x_res, u)).then_inc(stored, 16)
                sp.wait_ge(stored, 16 * NU)

        @block.gpsimd
        def _(pool):
            nc.gpsimd.memset(xt[:, :, :, 0:1], 0.0).then_inc(zero_ready, 1)
            pool.wait_ge(zero_ready, 1)

            def difference(u, par):
                pool.wait_ge(xt_ready, u + 1)
                nc.gpsimd.tensor_tensor(seqs(diff[:, par, :]), xt[:, par, :, 1:SEQ + 1], xt[:, par, :, 0:SEQ],
                                        ALU.subtract).then_inc(diff_ready, 1)

            front.gpsimd_rstd(pool, 0)
            difference(0, 0)
            front.gpsimd_rstd(pool, 1)

            def body(u, par, first, last):
                if not last:
                    difference(u + 1, 1 - par)
                if is_unit(u + 2):
                    front.gpsimd_rstd(pool, u + 2)

            over_units(pool, body)

        @block.vector
        def _(dve):
            front.vector_stats(dve, 0)
            front.vector_normalise(dve, 0, True)
            dve.wait_ge(weights_loaded, 5 * 16)

            def gate(u, par):
                dve.wait_ge(tanh_ready, u + 1)
                dve.wait_ge(v_ready, u + 1)
                after(dve, x_ready, u)
                nc.vector.scalar_tensor_tensor(gated[:], tanh_r[:, par, :], 1.0, ps_v[:], ALU.add,
                                               ALU.mult).then_inc(gated_ready, 1)
                dve.wait_ge(gated_ready, u + 1)
                nc.vector.scalar_tensor_tensor(unit_cols(x_res, u), gated[:], 0.5, unit_cols(x_res, u),
                                               ALU.mult, ALU.add).then_inc(x_ready, 1)

            front.vector_stats(dve, 1)

            def body(u, par, first, last):
                if not last:
                    front.vector_normalise(dve, u + 1, False)
                dve.wait_ge(diff_ready, u + 1)
                after(dve, rk_ready, u)
                nc.vector.scalar_tensor_tensor(seqs(xr[:]), seqs(diff[:, par, :]), mu_r[:], xt[:, par, :, 0:SEQ],
                                               ALU.mult, ALU.add)
                nc.vector.scalar_tensor_tensor(seqs(xk[:]), seqs(diff[:, par, :]), mu_k[:], xt[:, par, :, 0:SEQ],
                                               ALU.mult, ALU.add).then_inc(mix_ready, 1)
                if not first:
                    gate(u - 1, 1 - par)
                if is_unit(u + 2):
                    front.vector_stats(dve, u + 2)

            over_units(dve, body)
            gate(NU - 1, 1)

        @block.tensor
        def _(pe):
            front.tensor_transpose(pe, 0)
            pe.wait_ge(weights_loaded, 5 * 16)

            def gate(u, par):
                pe.wait_ge(k_act_ready, u + 1)
                for j in range(TU):
                    op = nc.tensor.matmul(ps_v[:, j * P:(j + 1) * P], k_act[:, par, j * P:(j + 1) * P], wv[:],
                                          start=True, stop=True)
                op.then_inc(v_ready, 1)

            def body(u, par, first, last):
                if not last:
                    pe.wait_ge(xt_ready, u + 1)
                    front.tensor_transpose(pe, u + 1)
                if not first:
                    after(pe, gated_ready, u - 1)
                    gate(u - 1, 1 - par)
                after(pe, tanh_ready, u)
                after(pe, relu_ready, u)
                pe.wait_ge(mix_ready, u + 1)
                nc.tensor.matmul(ps_k[:], wk[:], xk[:], start=True, stop=True).then_inc(k_ready, 1)
                for j in range(TU):
                    op = nc.tensor.matmul(ps_r[:, j * P:(j + 1) * P], xr[:, j * P:(j + 1) * P], wr[:],
                                          start=True, stop=True)
                op.then_inc(rk_ready, 1)

            over_units(pe, body)
            pe.wait_ge(gated_ready, NU - 1)
            gate(NU - 1, 1)

        @block.scalar
        def _(act):
            def copy_xt(u, par):
                act.wait_ge(front.xn_transposed, u + 1)
                after(act, mix_ready, u - 1)
                nc.scalar.copy(xt[:, par, :, 1:SEQ + 1], seqs(front.ps_t[:])).then_inc(xt_ready, 1)

            act.wait_ge(zero_ready, 1)
            copy_xt(0, 0)

            def body(u, par, first, last):
                if not last:
                    copy_xt(u + 1, 1 - par)
                act.wait_ge(k_ready, u + 1)
                nc.scalar.activation(relu_k[:], ps_k[:], ACT.Relu).then_inc(relu_ready, 1)
                act.wait_ge(relu_ready, u + 1)
                after(act, v_ready, u - 1)
                nc.scalar.activation(k_act[:, par, :], relu_k[:], ACT.Square).then_inc(k_act_ready, 1)
                act.wait_ge(rk_ready, u + 1)
                after(act, gated_ready, u - 1)
                nc.scalar.activation(tanh_r[:, par, :], ps_r[:], ACT.Tanh, scale=0.5).then_inc(tanh_ready, 1)

            over_units(act, body)
def attention_layer(nc, layer, x_res, ident, neg_half, eps, d):
    TS = SEQ // P
    HB = 4
    NBK = 2
    HS = HB * NBK
    NSL = H // HS
    BC = HB * HD * HE
    D = H * HD
    with ExitStack() as ctx:
        m = Memory(nc, ctx, layer)
        front = Front(nc, m, x_res, ident, neg_half, eps)
        ps_qkv = m.ps("ps_qkv", [P, TS, 512])
        ps_sum = m.ps("ps_sum", [P, 2, NBK, 512])
        ps_o = m.ps("ps_o", [P, UC])
        w_qkv, w_o = m.sb("w_qkv", [P, 3 * D]), m.sb("w_o", [P, P])
        triangle, ones = m.sb("triangle", [P, P]), m.sb("ones", [P, P])
        att_eps = m.sb("att_eps", [P, 1])
        xt = m.sb("xt", [P, 2, UC])
        exp_qk, exp_min = m.sb("exp_qk", [P, TS, 2 * D]), m.sb("exp_min", [P, TS, 2 * D])
        qk = m.sb("qk", [P, 2, TS, 2 * D])
        v_one = m.sb("v_one", [P, 2, TS, H, HE])
        kv = m.sb("kv", [P, 2, TS, H, HD, HE])
        prod = m.sb("prod", [P, 2, H, HD, HE])
        num_den = m.sb("num_den", [P, TS, H, HE])
        inv_den = m.sb("inv_den", [P, TS, H])
        att = m.sb("att", [P, 2, TU, D])
        att_t = m.sb("att_t", [P, UC])
        x_weights_loaded = m.sem("weights_loaded")
        constants_ready = m.sem("constants_ready")
        xt_ready = m.sem("xt_ready")
        qkv_ready, v_ready, min_ready, qk_ready = (
            m.sem(n) for n in ("qkv_ready", "v_ready", "min_ready", "qk_ready"))
        kv_ready = m.sem("kv_ready")
        sum_ready, prod_ready = m.sem("sum_ready"), m.sem("prod_ready")
        reduced, inv_ready, att_ready = (
            m.sem(n) for n in ("reduced", "inv_ready", "att_ready"))
        att_transposed, att_t_ready, out_ready, x_ready = (
            m.sem(n) for n in ("att_transposed", "att_t_ready", "out_ready", "x_ready"))
        block = ctx.enter_context(nc.Block())

        @block.sync
        def _(sp):
            sp.dma_start(w_qkv[:], d["W_qkvT"]).then_inc(x_weights_loaded, 16)
            sp.dma_start(w_o[:], d["W_oT"]).then_inc(x_weights_loaded, 16)

        WEIGHTS = 2 * 16

        @block.gpsimd
        def _(pool):
            nc.gpsimd.memset(att_eps[:], ATT_EPS)
            nc.gpsimd.memset(v_one[:, :, :, :, HD:HE], 1.0)
            nc.gpsimd.memset(ones[:], 1.0)
            nc.gpsimd.memset(triangle[:], 1.0).then_inc(constants_ready, 1)
            pool.wait_ge(constants_ready, 1)
            nc.gpsimd.affine_select(out=triangle[:], in_=triangle[:], compare_op=ALU.is_ge, fill=0.0, base=0,
                                    pattern=[[1, P]], channel_multiplier=-1).then_inc(constants_ready, 1)

            def outer(u, s):
                pool.wait_ge(v_ready, 2 * u + s + 1)
                pool.wait_ge(qk_ready, 2 * u + s + 1)
                for t in range(TS):
                    after(pool, sum_ready, (2 * u + s - 1) * TS * NSL)
                    k = qk[:, s, t, D:2 * D].rearrange("p (h d) -> p h d", h=H).unsqueeze(3)
                    v = v_one[:, s, t].unsqueeze(2)
                    nc.gpsimd.tensor_tensor(kv[:, s, t], k.broadcast_to([P, H, HD, HE]),
                                            v.broadcast_to([P, H, HD, HE]), ALU.mult).then_inc(kv_ready, 1)

            front.gpsimd_rstd(pool, 0)
            outer(0, 0)

            def body(u, par, first, last):
                if not last:
                    front.gpsimd_rstd(pool, u + 1)
                outer(u, 1)
                if not last:
                    outer(u + 1, 0)

            over_units(pool, body)

        @block.vector
        def _(dve):
            def features(u, s):
                dve.wait_ge(v_ready, 2 * u + s + 1)
                nc.vector.tensor_scalar(exp_min[:], exp_qk[:], 1.0, None, ALU.min).then_inc(min_ready, 1)
                dve.wait_ge(min_ready, 2 * u + s + 1)
                nc.vector.scalar_tensor_tensor(qk[:, s], ps_qkv[:, :, 0:2 * D], 0.0, exp_min[:], ALU.max,
                                               ALU.add).then_inc(qk_ready, 1)

            def contract(u, s):
                for t in range(TS):
                    for n in range(NSL):
                        dve.wait_ge(sum_ready, ((2 * u + s) * TS + t) * NSL + n + 1)
                        sums = ps_sum[:, n % 2, :, 0:BC].rearrange("p b (x e) -> p b x e", e=HE)
                        q = qk[:, s, t, n * HS * HD:(n + 1) * HS * HD].rearrange("p (b x) -> p b x", b=NBK)
                        out = prod[:, t, n * HS:(n + 1) * HS].rearrange("p (b h) d e -> p b (h d) e", b=NBK)
                        nc.vector.tensor_tensor(out, sums, q.unsqueeze(3).broadcast_to([P, NBK, HB * HD, HE]),
                                                ALU.mult).then_inc(prod_ready, 1)
                for t in range(TS):
                    dve.wait_ge(prod_ready, ((2 * u + s) * TS + t + 1) * NSL)
                    op = nc.vector.tensor_reduce(num_den[:, t], prod[:, t].rearrange("p h d e -> p h e d"), AX_X,
                                                 ALU.add)
                op.then_inc(reduced, 1)
                dve.wait_ge(reduced, 2 * u + s + 1)
                nc.vector.reciprocal(inv_den[:], num_den[:, :, :, HD]).then_inc(inv_ready, 1)
                after(dve, att_transposed, u - 1)
                dve.wait_ge(inv_ready, 2 * u + s + 1)

            def divide(u, s, par):
                out = att[:, par, s * TS:(s + 1) * TS].rearrange("p t (h e) -> p (t h) e", h=H)
                nc.vector.tensor_tensor(out, num_den[:, :, :, 0:HD].rearrange("p t h e -> p (t h) e"),
                                        inv_den[:].rearrange("p t h -> p (t h)").unsqueeze(2)
                                        .broadcast_to([P, TS * H, HD]), ALU.mult).then_inc(att_ready, 1)

            def add_out(u):
                dve.wait_ge(out_ready, u + 1)
                nc.vector.tensor_tensor(unit_cols(x_res, u), ps_o[:], unit_cols(x_res, u),
                                        ALU.add).then_inc(x_ready, 1)

            front.vector_stats(dve, 0)
            front.vector_normalise(dve, 0, True)
            dve.wait_ge(constants_ready, 2)
            features(0, 0)

            def body(u, par, first, last):
                if not last:
                    front.vector_stats(dve, u + 1)
                features(u, 1)
                if not last:
                    front.vector_normalise(dve, u + 1, False)
                contract(u, 0)
                divide(u, 0, par)
                if not last:
                    features(u + 1, 0)
                if not first:
                    add_out(u - 1)
                contract(u, 1)
                divide(u, 1, par)

            over_units(dve, body)
            add_out(NU - 1)

        @block.tensor
        def _(pe):
            def project(u, s, par):
                pe.wait_ge(xt_ready, u + 1)
                after(pe, qk_ready, 2 * u + s)
                for t in range(TS):
                    j = s * TS + t
                    op = nc.tensor.matmul(ps_qkv[:, t, 0:3 * D], xt[:, par, j * P:(j + 1) * P], w_qkv[:],
                                          start=True, stop=True)
                op.then_inc(qkv_ready, 1)

            def sums(u, s):
                for t in range(TS):
                    for n in range(NSL):
                        slot = ((2 * u + s) * TS + t) * NSL + n
                        after(pe, prod_ready, slot - 1)
                        pe.wait_ge(kv_ready, (2 * u + s) * TS + t + 1)
                        for b in range(NBK):
                            h = n * HS + b * HB
                            for tt in range(t + 1):
                                op = nc.tensor.matmul(
                                    ps_sum[:, n % 2, b, 0:BC], (triangle if tt == t else ones)[:],
                                    kv[:, s, tt, h:h + HB].rearrange("p h d e -> p (h d e)"),
                                    start=tt == 0, stop=tt == t)
                        op.then_inc(sum_ready, 1)

            def transpose_att(u, par):
                pe.wait_ge(att_ready, 2 * u + 2)
                after(pe, x_ready, u)
                for j in range(TU):
                    op = nc.tensor.transpose(ps_o[:, j * P:(j + 1) * P], att[:, par, j], ident[:])
                op.then_inc(att_transposed, 1)

            def project_out(u):
                pe.wait_ge(att_t_ready, u + 1)
                for j in range(TU):
                    op = nc.tensor.matmul(ps_o[:, j * P:(j + 1) * P], att_t[:, j * P:(j + 1) * P], w_o[:],
                                          start=True, stop=True)
                op.then_inc(out_ready, 1)

            front.tensor_transpose(pe, 0)
            pe.wait_ge(x_weights_loaded, WEIGHTS)
            pe.wait_ge(constants_ready, 2)
            project(0, 0, 0)

            def body(u, par, first, last):
                project(u, 1, par)
                if not first:
                    transpose_att(u - 1, 1 - par)
                if not last:
                    pe.wait_ge(xt_ready, u + 1)
                    front.tensor_transpose(pe, u + 1)
                sums(u, 0)
                if not last:
                    project(u + 1, 0, 1 - par)
                if not first:
                    project_out(u - 1)
                sums(u, 1)

            over_units(pe, body)
            transpose_att(NU - 1, 1)
            project_out(NU - 1)

        @block.scalar
        def _(act):
            def copy_xt(u, par):
                act.wait_ge(front.xn_transposed, u + 1)
                after(act, qkv_ready, 2 * u - 2)
                nc.scalar.copy(xt[:, par], front.ps_t[:]).then_inc(xt_ready, 1)

            def take_qkv(u, s):
                act.wait_ge(qkv_ready, 2 * u + s + 1)
                after(act, min_ready, 2 * u + s)
                nc.scalar.activation(exp_qk[:], ps_qkv[:, :, 0:2 * D], ACT.Exp)
                after(act, kv_ready, (2 * u + s - 1) * TS)
                nc.scalar.copy(v_one[:, s, :, :, 0:HD],
                               ps_qkv[:, :, 2 * D:3 * D].rearrange("p t (h e) -> p t h e", h=H)).then_inc(v_ready, 1)

            def copy_att(u):
                act.wait_ge(att_transposed, u + 1)
                after(act, out_ready, u)
                nc.scalar.activation(att_t[:], ps_o[:], ACT.Identity, bias=att_eps[:]).then_inc(att_t_ready, 1)

            act.wait_ge(constants_ready, 2)
            copy_xt(0, 0)
            take_qkv(0, 0)

            def body(u, par, first, last):
                take_qkv(u, 1)
                if not first:
                    copy_att(u - 1)
                if not last:
                    copy_xt(u + 1, 1 - par)
                    take_qkv(u + 1, 0)

            over_units(act, body)
            copy_att(NU - 1)


def mamba_layer(nc, layer, x_res, ident, neg_half, eps, d):
    NI, NG = 16, 8
    ND, NSC, NBR, NBS = 4, 8, 2, 4
    GS = 2
    BROWS = (0, 32, 64)
    NB = BROWS[-1] + NS
    LIM_SIG = 2.0 ** 60
    LIM_EXP = 2.0 ** 43
    LN_LIM = 43 * 0.6931471805599453
    with ExitStack() as ctx:
        m = Memory(nc, ctx, layer)
        front = Front(nc, m, x_res, ident, neg_half, eps)
        bank_a = front.ps_t
        bank_b = m.ps("bank_b", [P, UC])
        ps_y = m.ps("ps_y", [P, DI, UC])
        ps_br = m.ps("ps_br", [P, NBR, GS, UC])

        w_in = m.sb("w_in", [P, 2 * DI * P])
        conv_w = m.sb("conv_w", [P, TAPS, DI * P])
        w_tap = m.sb("w_tap", [P, TAPS, DI * P])
        w_dt = m.sb("w_dt", [P, DI, DI * P])
        w_b = m.sb("w_b", [P, DI, NB])
        w_out = m.sb("w_out", [P, DI, P])
        conv_b, b_dt, b_dt_lim, d_skip = (m.sb(n, [P, DI]) for n in ("conv_b", "b_dt", "b_dt_lim", "d_skip"))
        a_neg = m.sb("a_neg", [P, DI, NS])
        select = m.sb("select", [NB, NS, P], BF16)

        xt = m.sb("xt", [P, SU, SEQ + TAPS - 1])
        c_in, c_sig = m.sb("c_in", [P, DI, UC]), m.sb("c_sig", [P, DI, UC])
        z_in, z_sig = m.sb("z_in", [P, DI, UC]), m.sb("z_sig", [P, DI, UC])
        dt_exp, dt_over = m.sb("dt_exp", [P, DI, UC]), m.sb("dt_over", [P, DI, UC])
        b_parts = m.sb("b_parts", [NB, 2, UC], BF16)
        b_rest = m.sb("b_rest", [NB, UC])
        b_mid = m.sb("b_mid", [NB, UC], BF16)
        xc = m.sb("xc", [P, 2, DI, UC])
        z_gate = m.sb("z_gate", [P, 2, DI, UC])
        delta = m.sb("delta", [P, 2, DI, UC])
        dx = m.sb("dx", [P, 2, DI, UC])
        decay = m.sb("decay", [P, ND, GS, SU, SEQ])
        states = m.sb("states", [P, NSC, GS, UC])
        b_all = m.sb("b_all", [P, NBS, GS, UC])
        y_sum = m.sb("y_sum", [P, DI, UC])
        y_gated = m.sb("y_gated", [P, DI, UC])

        weights_loaded = m.sem("weights_loaded")
        b_zeroed = m.sem("b_zeroed")
        w_b_loaded = m.sem("w_b_loaded")
        pool_ready = m.sem("pool_ready")
        a_exp_ready = m.sem("a_exp_ready")
        a_ready = m.sem("a_ready")
        b_lim_ready = m.sem("b_lim_ready")
        w_tap_ready = m.sem("w_tap_ready")
        decay_ready, driven, scanned, read_out, reduced = (
            m.sem(n) for n in ("decay_ready", "driven", "scanned", "read_out", "reduced"))
        br_ready, b_all_ready = m.sem("br_ready"), m.sem("b_all_ready")
        (xt_ready, c0_ready, c1_ready, c0_copied, c1_copied, c_exp, c_lim, c_ln, c_sig_ready, xc_ready,
         bm_ready, b_hi_ready, b_rest_ready, b_mid_ready, b_parts_ready,
         dt0_ready, dt1_ready, dt0_taken, dt1_taken, dt_lim, dt_ln, delta_ready, dx_ready,
         z0_ready, z1_ready, z0_copied, z1_copied, z_exp, z_lim, z_ln, z_sig_ready, gate_ready,
         y_taken, y_ready, out_ready, x_ready) = (m.sem(n) for n in (
             "xt_ready", "c0_ready", "c1_ready", "c0_copied", "c1_copied", "c_exp", "c_lim", "c_ln",
             "c_sig_ready", "xc_ready", "bm_ready", "b_hi_ready", "b_rest_ready", "b_mid_ready",
             "b_parts_ready", "dt0_ready", "dt1_ready", "dt0_taken", "dt1_taken", "dt_lim", "dt_ln",
             "delta_ready", "dx_ready", "z0_ready", "z1_ready", "z0_copied", "z1_copied", "z_exp", "z_lim",
             "z_ln", "z_sig_ready", "gate_ready", "y_taken", "y_ready", "out_ready", "x_ready"))
        block = ctx.enter_context(nc.Block())

        @block.sync
        def _(sp):
            loads = ((w_in, d["W_in"]), (conv_w, d["conv_w"].partition_broadcast(P)), (conv_b, d["conv_b"]),
                     (w_dt, d["W_dt"]), (b_dt, d["b_dt"]), (a_neg, d["A_log"]), (d_skip, d["Dp"]),
                     (w_out, d["W_out"]))
            for dst, src in loads:
                sp.dma_start(dst[:], src).then_inc(weights_loaded, 16)
            sp.wait_ge(b_zeroed, 1)
            for row in BROWS:
                sp.dma_start(w_b[:, :, row:row + NS], d["W_xproj"][:, :, NS:2 * NS]).then_inc(w_b_loaded, 16)

        WEIGHTS = 8 * 16

        @block.gpsimd
        def _(pool):
            nc.gpsimd.memset(w_b[:], 0.0).then_inc(b_zeroed, 1)
            nc.gpsimd.memset(xt[:, :, 0:TAPS - 1], 0.0)
            nc.gpsimd.memset(decay[:, :, :, :, 0:1], 0.0)
            nc.gpsimd.memset(select[:], 0.0).then_inc(pool_ready, 1)
            pool.wait_ge(pool_ready, 1)
            for n, row in enumerate(BROWS):
                nc.gpsimd.affine_select(out=select[:], in_=select[:], compare_op=ALU.not_equal, fill=1.0,
                                        base=-row, pattern=[[-1, NS], [0, P]],
                                        channel_multiplier=1).then_inc(pool_ready, 1)
                pool.wait_ge(pool_ready, n + 2)

            front.gpsimd_rstd(pool, 0)
            front.gpsimd_rstd(pool, 1)

            def take_gate(u, par):
                pool.wait_ge(z_sig_ready, u + 1)
                after(pool, y_ready, u - 1)
                nc.gpsimd.tensor_tensor(z_gate[:, par], z_in[:], z_sig[:], ALU.mult).then_inc(gate_ready, 1)

            def gate_y(u, par):
                pool.wait_ge(y_taken, u + 1)
                after(pool, out_ready, u)
                pool.wait_ge(gate_ready, u + 1)
                nc.gpsimd.tensor_tensor(y_gated[:], y_sum[:], z_gate[:, par], ALU.mult).then_inc(y_ready, 1)

            take_gate(0, 0)

            def body(u, par, first, last):
                for k in range(NI):
                    g, slot = k // 2, k % NSC
                    pool.wait_ge(b_all_ready, u * NG + g + 1)
                    pool.wait_ge(scanned, u * NI + k + 1)
                    nc.gpsimd.tensor_tensor(states[:, slot, :, :], states[:, slot, :, :], b_all[:, g % NBS, :, :],
                                            ALU.mult).then_inc(read_out, 1)
                    if k == 1 and is_unit(u + 2):
                        front.gpsimd_rstd(pool, u + 2)
                    if k == 5 and not first:
                        gate_y(u - 1, 1 - par)
                    if k == 14 and not last:
                        take_gate(u + 1, 1 - par)

            over_units(pool, body)
            gate_y(NU - 1, 1)

        @block.vector
        def _(dve):
            front.vector_stats(dve, 0)
            front.vector_normalise(dve, 0, True)
            dve.wait_ge(weights_loaded, WEIGHTS)
            nc.vector.tensor_scalar(b_dt_lim[:], b_dt[:], LN_LIM, None, ALU.subtract).then_inc(b_lim_ready, 1)
            for t in range(TAPS):
                op = nc.vector.tensor_tensor(w_tap[:, t, :], w_in[:, 0:DI * P], conv_w[:, t, :], ALU.mult)
            op.then_inc(w_tap_ready, 1)

            def limit(buffer, ready, limited, u, bound):
                dve.wait_ge(ready, u + 1)
                nc.vector.tensor_scalar(buffer[:], buffer[:], bound, None, ALU.min).then_inc(limited, 1)

            def take_xc(u, par):
                dve.wait_ge(c_sig_ready, u + 1)
                nc.vector.tensor_tensor(xc[:, par], c_in[:], c_sig[:], ALU.mult).then_inc(xc_ready, 1)

            def take_b_rest(u, par):
                dve.wait_ge(b_hi_ready, u + 1)
                nc.vector.tensor_tensor(b_rest[:], bank_a[0:NB, :], b_parts[:, par, :],
                                        ALU.subtract).then_inc(b_rest_ready, 1)

            def take_b_low(u, par):
                dve.wait_ge(b_mid_ready, u + 1)
                nc.vector.tensor_tensor(b_parts[BROWS[2]:NB, par, :], b_rest[BROWS[2]:NB, :],
                                        b_mid[BROWS[2]:NB, :], ALU.subtract).then_inc(b_parts_ready, 1)

            def take_delta(u, par):
                dve.wait_ge(dt_ln, u + 1)
                nc.vector.tensor_tensor(delta[:, par], dt_exp[:], dt_over[:], ALU.add).then_inc(delta_ready, 1)
                dve.wait_ge(delta_ready, u + 1)
                nc.vector.tensor_tensor(dx[:, par], delta[:, par], xc[:, par], ALU.mult).then_inc(dx_ready, 1)

            def drive(u, par, k):
                g, h, slot = k // 2, k % 2, k % NSC
                dve.wait_ge(b_all_ready, u * NG + g + 1)
                after(dve, reduced, u * NI + k - NSC + 1)
                if k == 0:
                    dve.wait_ge(dx_ready, u + 1)
                nc.vector.tensor_tensor(states[:, slot, :, :],
                                        dx[:, par, h, :].unsqueeze(1).broadcast_to([P, GS, UC]),
                                        ps_br[:, g % NBR, :, :], ALU.mult).then_inc(driven, 1)

            def scan(u, k):
                slot = k % NSC
                dve.wait_ge(decay_ready, u * NI + k + 1)
                dve.wait_ge(driven, u * NI + k + 1)
                flat = states[:, slot, :, :].rearrange("p n c -> p (n c)")
                nc.vector.tensor_tensor_scan(flat, decay[:, k % ND].rearrange("p n s t -> p (n s t)"), flat,
                                             0.0, ALU.mult, ALU.add).then_inc(scanned, 1)

            def take_y(u, par):
                dve.wait_ge(reduced, (u + 1) * NI)
                after(dve, y_ready, u)
                for h in range(DI):
                    op = nc.vector.scalar_tensor_tensor(y_sum[:, h, :], xc[:, par, h, :], d_skip[:, h:h + 1],
                                                        ps_y[:, h, :], ALU.mult, ALU.add)
                op.then_inc(y_taken, 1)

            def add_out(u):
                dve.wait_ge(out_ready, u + 1)
                nc.vector.tensor_tensor(unit_cols(x_res, u), bank_b[:], unit_cols(x_res, u),
                                        ALU.add).then_inc(x_ready, 1)

            limit(c_sig, c_exp, c_lim, 0, LIM_SIG)
            take_xc(0, 0)
            take_b_rest(0, 0)
            take_b_low(0, 0)
            limit(dt_exp, dt1_taken, dt_lim, 0, LIM_EXP)
            take_delta(0, 0)
            limit(z_sig, z_exp, z_lim, 0, LIM_SIG)
            front.vector_stats(dve, 1)
            front.vector_normalise(dve, 1, False)
            drive(0, 0, 0)

            def body(u, par, first, last):
                for k in range(NI):
                    if k == 4 and not first:
                        take_y(u - 1, 1 - par)
                    if k + 1 < NI:
                        drive(u, par, k + 1)
                    elif not last:
                        drive(u + 1, 1 - par, 0)
                    scan(u, k)
                    if k == 0 and is_unit(u + 2):
                        front.vector_stats(dve, u + 2)
                    if k == 3 and not last:
                        limit(c_sig, c_exp, c_lim, u + 1, LIM_SIG)
                    if k == 5 and not last:
                        take_xc(u + 1, 1 - par)
                    if k == 8 and not last:
                        take_b_rest(u + 1, 1 - par)
                    if k == 10 and not last:
                        take_b_low(u + 1, 1 - par)
                    if k == 10 and not last:
                        limit(dt_exp, dt1_taken, dt_lim, u + 1, LIM_EXP)
                    if k == 12 and not first:
                        add_out(u - 1)
                    if k == 9 and is_unit(u + 2):
                        front.vector_normalise(dve, u + 2, False)
                    if k == 12 and not last:
                        take_delta(u + 1, 1 - par)
                    if k == 11 and not last:
                        limit(z_sig, z_exp, z_lim, u + 1, LIM_SIG)

            over_units(dve, body)
            take_y(NU - 1, 1)
            add_out(NU - 1)

        @block.tensor
        def _(pe):
            def mm(out, lhsT, rhs, start, stop):
                return nc.tensor.matmul(out, lhsT, rhs, start=start, stop=stop)

            def transpose(u):
                after(pe, dt1_taken, u)
                front.tensor_transpose(pe, u)

            def conv(u, h):
                bank, sem = ((bank_b, c0_ready), (bank_a, c1_ready))[h]
                pe.wait_ge(xt_ready, u + 1)
                if h == 0:
                    after(pe, dt0_taken, u)
                    after(pe, x_ready, u - 2)
                for t in range(TAPS):
                    op = mm(seqs(bank[:]), w_tap[:, t, h * P:(h + 1) * P], xt[:, :, t:t + SEQ],
                            t == 0, t == TAPS - 1)
                op.then_inc(sem, 1)

            def b_matrix(u, par):
                pe.wait_ge(xc_ready, u + 1)
                pe.wait_ge(z0_copied, u + 1)
                for h in range(DI):
                    op = mm(bank_a[0:NB, :], w_b[:, h, :], xc[:, par, h, :], h == 0, h == DI - 1)
                op.then_inc(bm_ready, 1)

            def dt_matrix(u, par, h):
                bank, sem = ((bank_b, dt0_ready), (bank_a, dt1_ready))[h]
                if h == 0:
                    pe.wait_ge(z1_copied, u + 1)
                else:
                    pe.wait_ge(b_rest_ready, u + 1)
                for i in range(DI):
                    op = mm(bank[:], w_dt[:, i, h * P:(h + 1) * P], xc[:, par, i, :], i == 0, i == DI - 1)
                op.then_inc(sem, 1)

            def z_matrix(u, h):
                bank, sem = ((bank_a, z0_ready), (bank_b, z1_ready))[h]
                pe.wait_ge((c1_copied, c0_copied)[h], u + 1)
                mm(seqs(bank[:]), w_in[:, (DI + h) * P:(DI + h + 1) * P], xt[:, :, TAPS - 1:TAPS - 1 + SEQ],
                   True, True).then_inc(sem, 1)

            def replicate(u, par, g):
                if g == 0:
                    pe.wait_ge(b_parts_ready, u + 1)
                after(pe, driven, (u * NG + g - NBR + 1) * 2)
                after(pe, b_all_ready, u * NG + g - NBR + 1)
                for j in range(GS):
                    op = mm(ps_br[:, g % NBR, j, :], select[:, g * GS + j, :], b_parts[:, par, :], True, True)
                op.then_inc(br_ready, 1)

            def reduce(u, k):
                g, h, slot = k // 2, k % 2, k % NSC
                if k == 0:
                    after(pe, y_taken, u)
                pe.wait_ge(read_out, u * NI + k + 1)
                for j in range(GS):
                    n = g * GS + j
                    op = mm(ps_y[:, h, :], ident[:], states[:, slot, j, :], n == 0, n == NS - 1)
                op.then_inc(reduced, 1)

            def project_out(u, last):
                pe.wait_ge(y_ready, u + 1)
                pe.wait_ge(dt0_taken, NU if last else u + 3)
                for j in range(TU):
                    for h in range(DI):
                        op = mm(bank_b[:, j * P:(j + 1) * P], y_gated[:, h, j * P:(j + 1) * P], w_out[:, h, :],
                                h == 0, h == DI - 1)
                op.then_inc(out_ready, 1)

            transpose(0)
            pe.wait_ge(w_tap_ready, 1)
            pe.wait_ge(weights_loaded, WEIGHTS)
            pe.wait_ge(w_b_loaded, 16 * len(BROWS))
            conv(0, 0)
            conv(0, 1)
            z_matrix(0, 0)
            z_matrix(0, 1)
            b_matrix(0, 0)
            dt_matrix(0, 0, 0)
            dt_matrix(0, 0, 1)
            transpose(1)
            conv(1, 0)
            conv(1, 1)
            replicate(0, 0, 0)
            LAG = 4

            def body(u, par, first, last):
                for k in range(NI):
                    if k % 2 == 0:
                        if k < NI - 2:
                            replicate(u, par, k // 2 + 1)
                        elif not last:
                            replicate(u + 1, 1 - par, 0)
                    if k >= LAG:
                        reduce(u, k - LAG)
                    elif not first:
                        reduce(u - 1, NI - LAG + k)
                    if k == 3 and not last:
                        z_matrix(u + 1, 0)
                        z_matrix(u + 1, 1)
                    if k == 6 and not last:
                        b_matrix(u + 1, 1 - par)
                        dt_matrix(u + 1, 1 - par, 0)
                    if k == 8 and not last:
                        dt_matrix(u + 1, 1 - par, 1)
                    if k == 9 and not first:
                        project_out(u - 1, last)
                    if k == 11 and is_unit(u + 2):
                        transpose(u + 2)
                    if k == 14 and is_unit(u + 2):
                        conv(u + 2, 0)
                    if k == 15 and is_unit(u + 2):
                        conv(u + 2, 1)

            over_units(pe, body)
            for k in range(NI - LAG, NI):
                reduce(NU - 1, k)
            pe.wait_ge(x_ready, NU - 1)
            project_out(NU - 1, True)

        @block.scalar
        def _(act):
            act.add_instruction(mybir.InstLoadActFuncSet(act_func_set_id=EXP_LN_SET,
                                                         name=nc.get_next_instruction_name()))
            act.wait_ge(weights_loaded, WEIGHTS)
            nc.scalar.activation(a_neg[:], a_neg[:], ACT.Exp).then_inc(a_exp_ready, 1)
            act.wait_ge(a_exp_ready, 1)
            nc.scalar.mul(a_neg[:], a_neg[:], -1.0).then_inc(a_ready, 1)
            act.wait_ge(a_ready, 1)
            act.wait_ge(pool_ready, 1)
            act.wait_ge(b_lim_ready, 1)

            def copy_xt(u):
                act.wait_ge(front.xn_transposed, u + 1)
                after(act, z1_ready, u)
                nc.scalar.copy(xt[:, :, TAPS - 1:], seqs(bank_a[:])).then_inc(xt_ready, 1)

            def copy_c(u, h):
                bank, ready, copied = ((bank_b, c0_ready, c0_copied), (bank_a, c1_ready, c1_copied))[h]
                after(act, xc_ready, u)
                act.wait_ge(ready, u + 1)
                nc.scalar.activation(c_in[:, h, :], bank[:], ACT.Identity,
                                     bias=conv_b[:, h:h + 1]).then_inc(copied, 1)

            def exp_c(u):
                act.wait_ge(c0_copied, u + 1)
                act.wait_ge(c1_copied, u + 1)
                nc.scalar.activation(c_sig[:], c_in[:], ACT.Exp, scale=-1.0).then_inc(c_exp, 1)

            def sigmoid_c(u):
                act.wait_ge(c_lim, u + 1)
                nc.scalar.activation(c_sig[:], c_sig[:], ACT.Ln, bias=1.0).then_inc(c_ln, 1)
                act.wait_ge(c_ln, u + 1)
                nc.scalar.activation(c_sig[:], c_sig[:], ACT.Exp, scale=-1.0).then_inc(c_sig_ready, 1)

            def first_b_part(u, par):
                act.wait_ge(bm_ready, u + 1)
                after(act, br_ready, (u - 1) * NG)
                nc.scalar.copy(b_parts[:, par, :], bank_a[0:NB, :]).then_inc(b_hi_ready, 1)

            def second_b_part(u, par):
                act.wait_ge(b_rest_ready, u + 1)
                nc.scalar.copy(b_parts[BROWS[1]:BROWS[2], par, :], b_rest[BROWS[1]:BROWS[2], :])
                nc.scalar.copy(b_mid[BROWS[2]:NB, :], b_rest[BROWS[2]:NB, :]).then_inc(b_mid_ready, 1)

            def take_dt(u, h):
                bank, ready, taken = ((bank_b, dt0_ready, dt0_taken), (bank_a, dt1_ready, dt1_taken))[h]
                act.wait_ge(ready, u + 1)
                after(act, delta_ready, u)
                nc.scalar.activation(dt_exp[:, h, :], bank[:], ACT.Exp, bias=b_dt[:, h:h + 1])
                nc.scalar.activation(dt_over[:, h, :], bank[:], ACT.Relu,
                                     bias=b_dt_lim[:, h:h + 1]).then_inc(taken, 1)

            def ln_dt(u):
                act.wait_ge(dt_lim, u + 1)
                nc.scalar.activation(dt_exp[:], dt_exp[:], ACT.Ln, bias=1.0).then_inc(dt_ln, 1)

            def copy_z(u, h):
                bank, ready, copied = ((bank_a, z0_ready, z0_copied), (bank_b, z1_ready, z1_copied))[h]
                after(act, gate_ready, u)
                act.wait_ge(ready, u + 1)
                nc.scalar.copy(z_in[:, h, :], bank[:]).then_inc(copied, 1)

            def exp_z(u):
                act.wait_ge(z0_copied, u + 1)
                act.wait_ge(z1_copied, u + 1)
                nc.scalar.activation(z_sig[:], z_in[:], ACT.Exp, scale=-1.0).then_inc(z_exp, 1)

            def sigmoid_z(u):
                act.wait_ge(z_lim, u + 1)
                nc.scalar.activation(z_sig[:], z_sig[:], ACT.Ln, bias=1.0).then_inc(z_ln, 1)
                act.wait_ge(z_ln, u + 1)
                nc.scalar.activation(z_sig[:], z_sig[:], ACT.Exp, scale=-1.0).then_inc(z_sig_ready, 1)

            def exps(u, par, k):
                g, h = k // 2, k % 2
                after(act, scanned, u * NI + k - ND + 1)
                if k == 0:
                    act.wait_ge(delta_ready, u + 1)
                for j in range(GS):
                    n = g * GS + j
                    op = nc.scalar.activation(decay[:, k % ND, j, :, 1:SEQ], seqs(delta[:, par, h, :])[:, :, 1:SEQ],
                                              ACT.Exp, scale=a_neg[:, h, n:n + 1])
                op.then_inc(decay_ready, 1)

            def copy_b(u, g):
                act.wait_ge(br_ready, u * NG + g + 1)
                after(act, read_out, (u * NG + g - NBS + 1) * 2)
                nc.scalar.copy(b_all[:, g % NBS], ps_br[:, g % NBR]).then_inc(b_all_ready, 1)

            AHEAD = 3
            copy_xt(0)
            copy_c(0, 0)
            copy_c(0, 1)
            exp_c(0)
            copy_z(0, 0)
            copy_z(0, 1)
            sigmoid_c(0)
            first_b_part(0, 0)
            take_dt(0, 0)
            second_b_part(0, 0)
            take_dt(0, 1)
            ln_dt(0)
            exp_z(0)
            sigmoid_z(0)
            copy_xt(1)
            copy_c(1, 0)
            for k in range(AHEAD):
                exps(0, 0, k)
            copy_b(0, 0)

            def body(u, par, first, last):
                for k in range(NI):
                    if k + AHEAD < NI:
                        exps(u, par, k + AHEAD)
                    elif not last:
                        exps(u + 1, 1 - par, k + AHEAD - NI)
                    if k % 2 == 0:
                        if k < NI - 2:
                            copy_b(u, k // 2 + 1)
                        elif not last:
                            copy_b(u + 1, 0)
                    if k == 12 and is_unit(u + 2):
                        copy_xt(u + 2)
                    if k == 15 and is_unit(u + 2):
                        copy_c(u + 2, 0)
                    if last:
                        continue
                    if k == 1:
                        copy_c(u + 1, 1)
                    if k == 2:
                        exp_c(u + 1)
                    if k == 4:
                        sigmoid_c(u + 1)
                        copy_z(u + 1, 0)
                        copy_z(u + 1, 1)
                    if k == 7:
                        first_b_part(u + 1, 1 - par)
                    if k == 8:
                        take_dt(u + 1, 0)
                    if k == 9:
                        second_b_part(u + 1, 1 - par)
                        exp_z(u + 1)
                    if k == 10:
                        take_dt(u + 1, 1)
                    if k == 11:
                        ln_dt(u + 1)
                    if k == 12:
                        sigmoid_z(u + 1)

            over_units(act, body)



def load_stream(nc, x_res, x_dram):
    with nc.semaphore("x_loaded") as x_loaded, nc.Block() as block:
        @block.sync
        def _(sp):
            sp.dma_start(x_res[:], x_dram).then_inc(x_loaded, 16)
            sp.wait_ge(x_loaded, 16)


def constants(nc, ident, neg_half, eps):
    with nc.semaphore("zeroed") as zeroed, nc.Block() as block:
        @block.gpsimd
        def _(pool):
            nc.gpsimd.memset(neg_half[:], -0.5)
            nc.gpsimd.memset(eps[:], LN_EPS)
            nc.gpsimd.memset(ident[:], 0.0).then_inc(zeroed, 1)
            pool.wait_ge(zeroed, 1)
            nc.gpsimd.affine_select(out=ident[:], in_=ident[:], compare_op=ALU.not_equal, fill=1.0, base=0,
                                    pattern=[[-1, P]], channel_multiplier=1).then_inc(zeroed, 1)
            pool.wait_ge(zeroed, 2)


def hybrid_kernel(nc, d):
    with ExitStack() as ctx:
        x_res = ctx.enter_context(nc.sbuf_tensor("x_res", [P, NU, UC], F32))
        ident = ctx.enter_context(nc.sbuf_tensor("ident", [P, P], F32))
        neg_half = ctx.enter_context(nc.sbuf_tensor("neg_half", [P, TU], F32))
        eps = ctx.enter_context(nc.sbuf_tensor("eps", [P, TU], F32))
        constants(nc, ident, neg_half, eps)
        load_stream(nc, x_res, d["x"])
        ffn = [d[n] for n in ("W_rT", "W_kT", "W_vT", "mu_r", "mu_k")]
        if "att" in LAYERS:
            attention_layer(nc, "att", x_res, ident, neg_half, eps, d)
        if "ffn1" in LAYERS:
            ffn_layer(nc, "ffn1", x_res, ident, neg_half, eps, ffn, None)
        if "mamba" in LAYERS:
            mamba_layer(nc, "mamba", x_res, ident, neg_half, eps, d)
        ffn_layer(nc, "ffn2", x_res, ident, neg_half, eps, ffn, d["out"])


def kernel(**inputs):
    import numpy as np
    import concourse.bacc as bacc
    from concourse.bass_utils import run_bass_kernel_spmd

    def a(name):
        return np.asarray(inputs[name])

    def halves(w):
        return w.reshape(DI, P, -1).transpose(1, 0, 2)

    arrays = {
        "x": a("L0_attn_a_x").reshape(NU, TU, P, P).transpose(2, 0, 1, 3).reshape(P, NU, UC),
        "W_qkvT": np.concatenate([a("L0_attn_a_Wq").T, a("L0_attn_a_Wk").T, a("L0_attn_a_Wv").T], 1),
        "W_oT": a("L0_attn_a_Wo").T,
        "W_in": a("L0_attn_b_W_in"),
        "conv_w": a("L0_attn_b_conv_w")[:, 0, :].T,
        "conv_b": halves(a("L0_attn_b_conv_b"))[:, :, 0],
        "W_xproj": halves(a("L0_attn_b_W_xproj")),
        "W_dt": halves(a("L0_attn_b_W_dt")),
        "b_dt": halves(a("L0_attn_b_b_dt"))[:, :, 0],
        "A_log": halves(a("L0_attn_b_A_log")),
        "Dp": halves(a("L0_attn_b_Dp"))[:, :, 0],
        "W_out": halves(a("L0_attn_b_W_out")),
        "W_rT": a("L0_ffn_W_r").T, "W_kT": a("L0_ffn_W_k").T, "W_vT": a("L0_ffn_W_v").T,
        "mu_r": a("L0_ffn_mu_r").reshape(P, 1), "mu_k": a("L0_ffn_mu_k").reshape(P, 1),
    }
    nc = bacc.Bacc("TRN2", target_bir_lowering=False, num_devices=1)
    dram, feed = {}, {}
    for name, array in arrays.items():
        array = np.ascontiguousarray(array)
        feed[f"in_{name}"] = array
        dram[name] = nc.dram_tensor(f"in_{name}", array.shape, mybir.dt.from_np(array.dtype),
                                    kind="ExternalInput").ap()
    dram["out"] = nc.dram_tensor("out_x", (P, NU, UC), F32, kind="ExternalOutput").ap()
    hybrid_kernel(nc, dram)
    got = run_bass_kernel_spmd(nc, [feed], core_ids=[0]).results[0]["out_x"]
    return got.reshape(P, NU, TU, P).transpose(1, 2, 0, 3).reshape(NSEQ, SEQ, P)
```

```python
from contextlib import ExitStack

import concourse.bass as bass
from concourse import mybir

P = 128
SEQ = 256
NSEQ = 32
SU = 2
UC = SU * SEQ
TU = UC // P
NU = NSEQ // SU
H, HD = 16, 8
HE = HD + 1
DI = 2
NS = 16
HEAD = 2
TAPS = 4
LN_EPS, ATT_EPS = 1e-5, 1e-12

F32, BF16 = mybir.dt.float32, mybir.dt.bfloat16
ALU = mybir.AluOpType
ACT = mybir.ActivationFunctionType
AX_X = mybir.AxisListType.X
LAYERS = ("att", "ffn1", "mamba", "ffn2")
BROWS = (0, 32, 64)
NB = BROWS[-1] + NS
EXP_LN_SET = 6


def over_units(eng, body):
    body(0, 0, True, False)
    body(1, 1, False, False)
    with eng.Fori(0, (NU - 4) // 2) as i:
        body(i * 2 + 2, 0, False, False)
        body(i * 2 + 3, 1, False, False)
    body(NU - 2, 0, False, False)
    body(NU - 1, 1, False, True)


def is_unit(u):
    return not isinstance(u, int) or u < NU


def after(eng, sem, count):
    if not isinstance(count, int) or count > 0:
        eng.wait_ge(sem, count)


class Weights:

    def __init__(self, nc, ctx, layer, shapes):
        self.tensors = {name: ctx.enter_context(nc.sbuf_tensor(name, shape, F32)) for name, shape in shapes.items()}
        self.loaded = ctx.enter_context(nc.semaphore(f"{layer}_weights_loaded"))
        self.loads = 0

    def __getitem__(self, name):
        return self.tensors[name]

    def load(self, queue, destination, source):
        queue.dma_start(destination, source).then_inc(self.loaded, 16)
        self.loads += 1

    def await_on(self, eng):
        eng.wait_ge(self.loaded, 16 * self.loads)


class Memory:

    def __init__(self, nc, ctx, layer):
        self.nc, self.ctx, self.layer = nc, ctx, layer

    def sb(self, name, shape, dtype=F32):
        return self.ctx.enter_context(self.nc.sbuf_tensor(f"{self.layer}_{name}", shape, dtype))

    def ps(self, name, shape, dtype=F32):
        return self.ctx.enter_context(self.nc.psum_tensor(f"{self.layer}_{name}", shape, dtype))

    def sem(self, name):
        return self.ctx.enter_context(self.nc.semaphore(f"{self.layer}_{name}"))


def unit_cols(x_res, u, c0=0, c1=UC):
    return x_res[:, bass.ds(u, 1), c0:c1].rearrange("p o c -> p (o c)")


class Front:

    def __init__(self, nc, m, x_res, consts):
        self.nc, self.x_res, self.consts = nc, x_res, consts
        self.stats = m.sb("stats", [P, TU, 6])
        self.mean_var = m.sb("mean_var", [P, TU, 2])
        self.var_eps, self.neg_mean = m.sb("var_eps", [P, TU]), m.sb("neg_mean", [P, TU])
        self.rstd, self.shift = m.sb("rstd", [P, TU]), m.sb("shift", [P, TU])
        self.pad = m.sb("pad", [P, 1])
        self.xn = m.sb("xn", [P, UC])
        self.ps_t = m.ps("ps_t", [P, UC])
        self.stats_ready = m.sem("stats_ready")
        self.mean_ready = m.sem("mean_ready")
        self.eps_ready = m.sem("eps_ready")
        self.rstd_ready = m.sem("rstd_ready")
        self.shift_ready = m.sem("shift_ready")
        self.xn_ready = m.sem("xn_ready")
        self.xn_transposed = m.sem("xn_transposed")

    def vector_stats(self, dve, u):
        nc = self.nc
        after(dve, self.mean_ready, u)
        for j in range(TU):
            op = nc.vector.bn_stats(self.stats[:, j, :], unit_cols(self.x_res, u, j * P, (j + 1) * P))
        op.then_inc(self.stats_ready, 1)
        dve.wait_ge(self.stats_ready, u + 1)
        after(dve, self.shift_ready, u)
        nc.vector.memset(self.pad[:], 0.0)
        for j in range(TU):
            op = nc.vector.bn_aggr(self.mean_var[:, j, :], self.stats[:, j, :])
        op.then_inc(self.mean_ready, 1)

    def gpsimd_rstd(self, pool, u):
        nc, c = self.nc, self.consts
        pool.wait_ge(self.mean_ready, u + 1)
        after(pool, self.shift_ready, u)
        nc.gpsimd.tensor_tensor(self.var_eps[:], self.mean_var[:, :, 1], c["eps"][:], ALU.add)
        nc.gpsimd.tensor_tensor(self.neg_mean[:], self.mean_var[:, :, 0], c["neg_one"][:],
                                ALU.mult).then_inc(self.eps_ready, 1)
        after(pool, self.xn_ready, u)
        pool.wait_ge(self.eps_ready, u + 1)
        nc.gpsimd.tensor_tensor(self.rstd[:], self.var_eps[:], c["neg_half"][:],
                                ALU.pow).then_inc(self.rstd_ready, 1)
        pool.wait_ge(self.rstd_ready, u + 1)
        nc.gpsimd.tensor_tensor(self.shift[:], self.neg_mean[:], self.rstd[:],
                                ALU.mult).then_inc(self.shift_ready, 1)

    def scalar_normalise(self, act, u):
        nc = self.nc
        act.wait_ge(self.shift_ready, u + 1)
        after(act, self.xn_transposed, u)
        for j in range(TU):
            op = nc.scalar.activation(self.xn[:, j * P:(j + 1) * P],
                                      unit_cols(self.x_res, u, j * P, (j + 1) * P), ACT.Identity,
                                      bias=self.shift[:, j:j + 1], scale=self.rstd[:, j:j + 1])
        op.then_inc(self.xn_ready, 1)

    def tensor_transpose(self, pe, u):
        nc = self.nc
        pe.wait_ge(self.xn_ready, u + 1)
        for j in range(TU):
            op = nc.tensor.transpose(self.ps_t[:, j * P:(j + 1) * P], self.xn[:, j * P:(j + 1) * P],
                                     self.consts["ident"][:])
        op.then_inc(self.xn_transposed, 1)


def seqs(ap):
    return ap.rearrange("p (s t) -> p s t", s=SU)


def ffn_layer(nc, layer, x_res, consts, weights, out_dram):
    wr, wk, wv, mu_r, mu_k = (weights[n] for n in ("wr", "wk", "wv", "mu_r", "mu_k"))
    with ExitStack() as ctx:
        m = Memory(nc, ctx, layer)
        front = Front(nc, m, x_res, consts)
        xt = m.sb("xt", [P, 2, SU, SEQ + 1])
        diff = m.sb("diff", [P, 2, UC])
        xr, xk = m.sb("xr", [P, UC]), m.sb("xk", [P, UC])
        tanh_r = m.sb("tanh_r", [P, 2, UC])
        relu_k = m.sb("relu_k", [P, UC])
        k_act = m.sb("k_act", [P, 2, UC])
        gated = m.sb("gated", [P, UC])
        ps_r, ps_k, ps_v = (m.ps(n, [P, UC]) for n in ("ps_r", "ps_k", "ps_v"))
        zero_ready = m.sem("zero_ready")
        xt_ready = m.sem("xt_ready")
        diff_ready = m.sem("diff_ready")
        mix_ready = m.sem("mix_ready")
        k_ready = m.sem("k_ready")
        rk_ready = m.sem("rk_ready")
        tanh_ready = m.sem("tanh_ready")
        relu_ready = m.sem("relu_ready")
        k_act_ready = m.sem("k_act_ready")
        v_ready = m.sem("v_ready")
        gated_ready = m.sem("gated_ready")
        x_ready = m.sem("x_ready")
        stored = m.sem("stored")
        block = ctx.enter_context(nc.Block())

        @block.sync
        def _(sp):
            if out_dram is not None:
                with sp.Fori(0, NU) as u:
                    sp.wait_ge(x_ready, u + 1)
                    sp.dma_start(unit_cols(out_dram, u), unit_cols(x_res, u)).then_inc(stored, 16)
                sp.wait_ge(stored, 16 * NU)

        @block.gpsimd
        def _(pool):
            nc.gpsimd.memset(xt[:, :, :, 0:1], 0.0).then_inc(zero_ready, 1)
            pool.wait_ge(zero_ready, 1)

            def difference(u, par):
                pool.wait_ge(xt_ready, u + 1)
                nc.gpsimd.tensor_tensor(seqs(diff[:, par, :]), xt[:, par, :, 1:SEQ + 1], xt[:, par, :, 0:SEQ],
                                        ALU.subtract).then_inc(diff_ready, 1)

            front.gpsimd_rstd(pool, 0)
            difference(0, 0)
            front.gpsimd_rstd(pool, 1)

            def body(u, par, first, last):
                if is_unit(u + 2):
                    front.gpsimd_rstd(pool, u + 2)
                if not last:
                    difference(u + 1, 1 - par)

            over_units(pool, body)

        @block.vector
        def _(dve):
            front.vector_stats(dve, 0)
            weights.await_on(dve)

            def gate(u, par):
                dve.wait_ge(tanh_ready, u + 1)
                dve.wait_ge(v_ready, u + 1)
                after(dve, x_ready, u)
                nc.vector.scalar_tensor_tensor(gated[:], tanh_r[:, par, :], 1.0, ps_v[:], ALU.add,
                                               ALU.mult).then_inc(gated_ready, 1)
                dve.wait_ge(gated_ready, u + 1)
                nc.vector.scalar_tensor_tensor(unit_cols(x_res, u), gated[:], 0.5, unit_cols(x_res, u),
                                               ALU.mult, ALU.add).then_inc(x_ready, 1)

            front.vector_stats(dve, 1)

            def body(u, par, first, last):
                if is_unit(u + 2):
                    front.vector_stats(dve, u + 2)
                dve.wait_ge(diff_ready, u + 1)
                after(dve, rk_ready, u)
                nc.vector.scalar_tensor_tensor(seqs(xr[:]), seqs(diff[:, par, :]), mu_r[:], xt[:, par, :, 0:SEQ],
                                               ALU.mult, ALU.add)
                nc.vector.scalar_tensor_tensor(seqs(xk[:]), seqs(diff[:, par, :]), mu_k[:], xt[:, par, :, 0:SEQ],
                                               ALU.mult, ALU.add).then_inc(mix_ready, 1)
                if not first:
                    gate(u - 1, 1 - par)

            over_units(dve, body)
            gate(NU - 1, 1)

        @block.tensor
        def _(pe):
            front.tensor_transpose(pe, 0)
            weights.await_on(pe)

            def gate(u, par):
                pe.wait_ge(k_act_ready, u + 1)
                for j in range(TU):
                    op = nc.tensor.matmul(ps_v[:, j * P:(j + 1) * P], k_act[:, par, j * P:(j + 1) * P], wv[:],
                                          start=True, stop=True)
                op.then_inc(v_ready, 1)

            def body(u, par, first, last):
                if not last:
                    pe.wait_ge(xt_ready, u + 1)
                    front.tensor_transpose(pe, u + 1)
                if not first:
                    after(pe, gated_ready, u - 1)
                    gate(u - 1, 1 - par)
                after(pe, tanh_ready, u)
                after(pe, relu_ready, u)
                pe.wait_ge(mix_ready, u + 1)
                nc.tensor.matmul(ps_k[:], wk[:], xk[:], start=True, stop=True).then_inc(k_ready, 1)
                for j in range(TU):
                    op = nc.tensor.matmul(ps_r[:, j * P:(j + 1) * P], xr[:, j * P:(j + 1) * P], wr[:],
                                          start=True, stop=True)
                op.then_inc(rk_ready, 1)

            over_units(pe, body)
            pe.wait_ge(gated_ready, NU - 1)
            gate(NU - 1, 1)

        @block.scalar
        def _(act):
            def copy_xt(u, par):
                act.wait_ge(front.xn_transposed, u + 1)
                after(act, mix_ready, u - 1)
                nc.scalar.copy(xt[:, par, :, 1:SEQ + 1], seqs(front.ps_t[:])).then_inc(xt_ready, 1)

            act.wait_ge(zero_ready, 1)
            front.scalar_normalise(act, 0)
            copy_xt(0, 0)
            front.scalar_normalise(act, 1)

            def body(u, par, first, last):
                if not last:
                    copy_xt(u + 1, 1 - par)
                if is_unit(u + 2):
                    front.scalar_normalise(act, u + 2)
                act.wait_ge(k_ready, u + 1)
                nc.scalar.activation(relu_k[:], ps_k[:], ACT.Relu).then_inc(relu_ready, 1)
                act.wait_ge(relu_ready, u + 1)
                after(act, v_ready, u - 1)
                nc.scalar.activation(k_act[:, par, :], relu_k[:], ACT.Square).then_inc(k_act_ready, 1)
                act.wait_ge(rk_ready, u + 1)
                after(act, gated_ready, u - 1)
                nc.scalar.activation(tanh_r[:, par, :], ps_r[:], ACT.Tanh, scale=0.5).then_inc(tanh_ready, 1)

            over_units(act, body)


def attention_layer(nc, layer, x_res, consts, weights, x_head, x_rest):
    TS = SEQ // P
    HB = 4
    NBK = 2
    HS = HB * NBK
    NSL = H // HS
    BC = HB * HD * HE
    D = H * HD
    with ExitStack() as ctx:
        m = Memory(nc, ctx, layer)
        front = Front(nc, m, x_res, consts)
        ps_qkv = m.ps("ps_qkv", [P, TS, 512])
        ps_sum = m.ps("ps_sum", [P, 2, NBK, 512])
        ps_o = front.ps_t
        ps_carry = m.ps("ps_carry", [P, 512])
        KV, QT = slice(0, H * HE), slice(H * HE, H * HE + P)
        CARRY = slice(H * HE + P, 2 * H * HE + P)
        w_qkv, w_o = weights["w_qkv"], weights["w_o"]
        triangle = m.sb("triangle", [P, P])
        same_head = m.sb("same_head", [P, H, HE])
        att_eps = m.sb("att_eps", [P, 1])
        xt = m.sb("xt", [P, 2, UC])
        neg_qk, exp_qk = m.sb("neg_qk", [P, TS, 2 * D]), m.sb("exp_qk", [P, TS, 2 * D])
        qk = m.sb("qk", [P, 2, TS, 2 * D])
        v_one = m.sb("v_one", [P, 2, TS, H, HE])
        kv = m.sb("kv", [P, 2, TS, H, HD, HE])
        prod = m.sb("prod", [P, 2, H, HD, HE])
        total_q = m.sb("total_q", [P, H * HE + P])
        state = m.sb("state", [P, H * HE])
        num_den = m.sb("num_den", [P, TS, H, HE])
        inv_den = m.sb("inv_den", [P, TS, H])
        att = m.sb("att", [P, 2, TU, D])
        att_t = m.sb("att_t", [P, UC])
        constants_ready = m.sem("constants_ready")
        xt_ready = m.sem("xt_ready")
        qkv_ready, neg_ready, v_ready, exp_ready, qk_ready = (
            m.sem(n) for n in ("qkv_ready", "neg_ready", "v_ready", "exp_ready", "qk_ready"))
        kv_ready = m.sem("kv_ready")
        sum_ready, prod_ready = m.sem("sum_ready"), m.sem("prod_ready")
        total_ready, total_copied, state_ready, carry_ready, carried = (
            m.sem(n) for n in ("total_ready", "total_copied", "state_ready", "carry_ready", "carried"))
        reduced = m.sem("reduced")
        inv_ready, att_ready = m.sem("inv_ready"), m.sem("att_ready")
        att_transposed, att_t_ready, out_ready, x_ready = (
            m.sem(n) for n in ("att_transposed", "att_t_ready", "out_ready", "x_ready"))
        block = ctx.enter_context(nc.Block())

        @block.gpsimd
        def _(pool):
            nc.gpsimd.memset(att_eps[:], ATT_EPS)
            nc.gpsimd.memset(v_one[:, :, :, :, HD:HE], 1.0)
            nc.gpsimd.memset(same_head[:], 1.0)
            nc.gpsimd.memset(triangle[:], 1.0).then_inc(constants_ready, 1)
            pool.wait_ge(constants_ready, 1)
            nc.gpsimd.affine_select(out=triangle[:], in_=triangle[:], compare_op=ALU.is_ge, fill=0.0, base=0,
                                    pattern=[[1, P]], channel_multiplier=-1)
            nc.gpsimd.affine_select(out=same_head[:], in_=same_head[:], compare_op=ALU.is_ge, fill=0.0, base=0,
                                    pattern=[[-HD, H], [0, HE]], channel_multiplier=1).then_inc(constants_ready, 1)
            pool.wait_ge(constants_ready, 2)
            nc.gpsimd.affine_select(out=same_head[:], in_=same_head[:], compare_op=ALU.is_ge, fill=0.0,
                                    base=HD - 1, pattern=[[HD, H], [0, HE]],
                                    channel_multiplier=-1).then_inc(constants_ready, 1)

            def outer(u, s):
                pool.wait_ge(v_ready, 2 * u + s + 1)
                pool.wait_ge(qk_ready, 2 * u + s + 1)
                for t in range(TS):
                    after(pool, sum_ready, (2 * u + s - 1) * TS * NSL)
                    k = qk[:, s, t, D:2 * D].rearrange("p (h d) -> p h d", h=H).unsqueeze(3)
                    v = v_one[:, s, t].unsqueeze(2)
                    nc.gpsimd.tensor_tensor(kv[:, s, t], k.broadcast_to([P, H, HD, HE]),
                                            v.broadcast_to([P, H, HD, HE]), ALU.mult).then_inc(kv_ready, 1)

            def keep_heads(u, s):
                pool.wait_ge(total_copied, 2 * u + s + 1)
                after(pool, carry_ready, 2 * u + s)
                nc.gpsimd.tensor_tensor(state[:], total_q[:, KV], same_head[:].rearrange("p h e -> p (h e)"),
                                        ALU.mult).then_inc(state_ready, 1)

            def divide(u, s, par):
                if s == 0:
                    after(pool, att_transposed, u - 1)
                pool.wait_ge(inv_ready, 2 * u + s + 1)
                out = att[:, par, s * TS:(s + 1) * TS].rearrange("p t (h e) -> p (t h) e", h=H)
                nc.gpsimd.tensor_tensor(out, num_den[:, :, :, 0:HD].rearrange("p t h e -> p (t h) e"),
                                        inv_den[:].rearrange("p t h -> p (t h)").unsqueeze(2)
                                        .broadcast_to([P, TS * H, HD]), ALU.mult).then_inc(att_ready, 1)

            front.gpsimd_rstd(pool, 0)
            front.gpsimd_rstd(pool, 1)
            outer(0, 0)

            def body(u, par, first, last):
                if not first:
                    divide(u - 1, 1, 1 - par)
                keep_heads(u, 0)
                outer(u, 1)
                divide(u, 0, par)
                keep_heads(u, 1)
                if is_unit(u + 2):
                    front.gpsimd_rstd(pool, u + 2)
                if not last:
                    outer(u + 1, 0)

            over_units(pool, body)
            divide(NU - 1, 1, 1)

        @block.vector
        def _(dve):
            def features(u, s):
                q = 2 * u + s
                dve.wait_ge(exp_ready, q + 1)
                after(dve, kv_ready, (q - 1) * TS)
                nc.vector.scalar_tensor_tensor(qk[:, s], ps_qkv[:, :, 0:2 * D], 0.0, exp_qk[:], ALU.max,
                                               ALU.add).then_inc(qk_ready, 1)

            def multiply(u, s, t, n):
                dve.wait_ge(sum_ready, ((2 * u + s) * TS + t) * NSL + n + 1)
                sums = ps_sum[:, n % 2, :, 0:BC].rearrange("p b (x e) -> p b x e", e=HE)
                q = qk[:, s, t, n * HS * HD:(n + 1) * HS * HD].rearrange("p (b x) -> p b x", b=NBK)
                out = prod[:, t, n * HS:(n + 1) * HS].rearrange("p (b h) d e -> p b (h d) e", b=NBK)
                nc.vector.tensor_tensor(out, sums, q.unsqueeze(3).broadcast_to([P, NBK, HB * HD, HE]),
                                        ALU.mult).then_inc(prod_ready, 1)

            def reduce(u, s, t):
                dve.wait_ge(prod_ready, ((2 * u + s) * TS + t + 1) * NSL)
                after(dve, att_ready, 2 * u + s)
                nc.vector.tensor_reduce(num_den[:, t], prod[:, t].rearrange("p h d e -> p h e d"), AX_X,
                                        ALU.add).then_inc(reduced, 1)

            def invert(u, s):
                dve.wait_ge(reduced, (2 * u + s + 1) * TS)
                dve.wait_ge(carry_ready, 2 * u + s + 1)
                second = num_den[:, 1].rearrange("p h e -> p (h e)")
                nc.vector.tensor_tensor(second, ps_carry[:, CARRY], second, ALU.add).then_inc(carried, 1)
                dve.wait_ge(carried, 2 * u + s + 1)
                nc.vector.reciprocal(inv_den[:], num_den[:, :, :, HD]).then_inc(inv_ready, 1)

            def add_out(u):
                dve.wait_ge(out_ready, u + 1)
                nc.vector.tensor_tensor(unit_cols(x_res, u), ps_o[:], unit_cols(x_res, u),
                                        ALU.add).then_inc(x_ready, 1)

            dve.wait_ge(x_head, 16)
            front.vector_stats(dve, 0)
            front.vector_stats(dve, 1)
            dve.wait_ge(constants_ready, 3)
            features(0, 0)

            multiply(0, 0, 0, 0)

            def body(u, par, first, last):
                for s in range(SU):
                    if s == 1:
                        invert(u, 0)
                    elif not first:
                        invert(u - 1, 1)
                    multiply(u, s, 0, 1)
                    if s == 0 and first:
                        dve.wait_ge(x_rest, 16)
                    if s == 0 and is_unit(u + 2):
                        front.vector_stats(dve, u + 2)
                    if s == 1 and not first:
                        add_out(u - 1)
                    if s == 0:
                        features(u, 1)
                    elif not last:
                        features(u + 1, 0)
                    multiply(u, s, 1, 0)
                    reduce(u, s, 0)
                    multiply(u, s, 1, 1)
                    reduce(u, s, 1)
                    if s == 0:
                        multiply(u, 1, 0, 0)
                    elif not last:
                        multiply(u + 1, 0, 0, 0)

            over_units(dve, body)
            invert(NU - 1, 1)
            add_out(NU - 1)

        @block.tensor
        def _(pe):
            def project(u, s, par):
                pe.wait_ge(xt_ready, u + 1)
                after(pe, qk_ready, 2 * u + s)
                for t in range(TS):
                    j = s * TS + t
                    op = nc.tensor.matmul(ps_qkv[:, t, 0:3 * D], xt[:, par, j * P:(j + 1) * P], w_qkv[:],
                                          start=True, stop=True)
                op.then_inc(qkv_ready, 1)

            def sums(u, s, t, slots=range(NSL)):
                for n in slots:
                    slot = ((2 * u + s) * TS + t) * NSL + n
                    after(pe, prod_ready, slot - 1)
                    pe.wait_ge(kv_ready, (2 * u + s) * TS + t + 1)
                    for b in range(NBK):
                        h = n * HS + b * HB
                        op = nc.tensor.matmul(ps_sum[:, n % 2, b, 0:BC], triangle[:],
                                              kv[:, s, t, h:h + HB].rearrange("p h d e -> p (h d e)"),
                                              start=True, stop=True)
                    op.then_inc(sum_ready, 1)

            def total(u, s):
                q = 2 * u + s
                after(pe, carried, q)
                nc.tensor.matmul(ps_carry[:, KV], qk[:, s, 0, D:2 * D],
                                 v_one[:, s, 0].rearrange("p h e -> p (h e)"), start=True, stop=True)
                nc.tensor.transpose(ps_carry[:, QT], qk[:, s, 1, 0:D], consts["ident"][:]).then_inc(total_ready, 1)

            def carry(u, s):
                pe.wait_ge(state_ready, 2 * u + s + 1)
                nc.tensor.matmul(ps_carry[:, CARRY], total_q[:, QT], state[:], start=True, stop=True).then_inc(carry_ready, 1)

            def transpose_att(u, par, last):
                pe.wait_ge(att_ready, 2 * u + 2)
                after(pe, x_ready, u)
                pe.wait_ge(xt_ready, NU if last else u + 3)
                for j in range(TU):
                    op = nc.tensor.transpose(ps_o[:, j * P:(j + 1) * P], att[:, par, j], consts["ident"][:])
                op.then_inc(att_transposed, 1)

            def project_out(u):
                pe.wait_ge(att_t_ready, u + 1)
                for j in range(TU):
                    op = nc.tensor.matmul(ps_o[:, j * P:(j + 1) * P], att_t[:, j * P:(j + 1) * P], w_o[:],
                                          start=True, stop=True)
                op.then_inc(out_ready, 1)

            front.tensor_transpose(pe, 0)
            weights.await_on(pe)
            pe.wait_ge(constants_ready, 3)
            project(0, 0, 0)
            project(0, 1, 0)

            def body(u, par, first, last):
                sums(u, 0, 0)
                total(u, 0)
                if not last:
                    after(pe, x_ready, u - 1)
                    front.tensor_transpose(pe, u + 1)
                sums(u, 0, 1, (0,))
                carry(u, 0)
                if not first:
                    transpose_att(u - 1, 1 - par, last)
                sums(u, 0, 1, (1,))
                if not last:
                    project(u + 1, 0, 1 - par)
                sums(u, 1, 0)
                total(u, 1)
                if not first:
                    project_out(u - 1)
                sums(u, 1, 1, (0,))
                carry(u, 1)
                sums(u, 1, 1, (1,))
                if not last:
                    project(u + 1, 1, 1 - par)

            over_units(pe, body)
            transpose_att(NU - 1, 1, True)
            project_out(NU - 1)

        @block.scalar
        def _(act):
            def copy_xt(u, par):
                act.wait_ge(front.xn_transposed, u + 1)
                after(act, qkv_ready, 2 * u - 2)
                nc.scalar.copy(xt[:, par], front.ps_t[:]).then_inc(xt_ready, 1)

            def take_qkv(u, s):
                q = 2 * u + s
                act.wait_ge(qkv_ready, q + 1)
                after(act, exp_ready, q)
                nc.scalar.activation(neg_qk[:], ps_qkv[:, :, 0:2 * D], ACT.Relu, scale=-1.0).then_inc(neg_ready, 1)
                after(act, kv_ready, (q - 1) * TS)
                nc.scalar.copy(v_one[:, s, :, :, 0:HD],
                               ps_qkv[:, :, 2 * D:3 * D].rearrange("p t (h e) -> p t h e", h=H)).then_inc(v_ready, 1)
                act.wait_ge(neg_ready, q + 1)
                after(act, qk_ready, q)
                nc.scalar.activation(exp_qk[:], neg_qk[:], ACT.Exp, scale=-1.0).then_inc(exp_ready, 1)

            def copy_total(u, s):
                act.wait_ge(total_ready, 2 * u + s + 1)
                after(act, carry_ready, 2 * u + s)
                nc.scalar.copy(total_q[:], ps_carry[:, 0:H * HE + P]).then_inc(total_copied, 1)

            def copy_att(u):
                act.wait_ge(att_transposed, u + 1)
                after(act, out_ready, u)
                nc.scalar.activation(att_t[:], ps_o[:], ACT.Identity, bias=att_eps[:]).then_inc(att_t_ready, 1)

            act.wait_ge(constants_ready, 3)
            front.scalar_normalise(act, 0)
            copy_xt(0, 0)
            front.scalar_normalise(act, 1)
            take_qkv(0, 0)
            take_qkv(0, 1)

            def body(u, par, first, last):
                copy_total(u, 0)
                if not last:
                    copy_xt(u + 1, 1 - par)
                if not first:
                    copy_att(u - 1)
                if not last:
                    take_qkv(u + 1, 0)
                copy_total(u, 1)
                if is_unit(u + 2):
                    front.scalar_normalise(act, u + 2)
                if not last:
                    take_qkv(u + 1, 1)

            over_units(act, body)
            copy_att(NU - 1)


def mamba_layer(nc, layer, x_res, consts, weights):
    NI, NG = 16, 8
    ND, NSC, NBR, NBS = 4, 8, 2, 4
    GS = 2
    LIM_SIG = 2.0 ** 60
    LIM_EXP = 2.0 ** 43
    LN_LIM = 43 * 0.6931471805599453
    with ExitStack() as ctx:
        m = Memory(nc, ctx, layer)
        front = Front(nc, m, x_res, consts)
        bank_a = front.ps_t
        bank_b = m.ps("bank_b", [P, UC])
        ps_y = m.ps("ps_y", [P, DI, UC])
        ps_br = m.ps("ps_br", [P, NBR, GS, UC])

        w_in, conv_w, w_dt, w_b, w_out, conv_b, b_dt, d_skip, a_log = (weights[n] for n in (
            "w_in", "conv_w", "w_dt", "w_b", "w_out", "conv_b", "b_dt", "d_skip", "a_log"))
        w_tap = m.sb("w_tap", [P, TAPS, DI * P])
        b_dt_lim = m.sb("b_dt_lim", [P, DI])
        a_exp = m.sb("a_exp", [P, DI, NS])
        a_neg = m.sb("a_neg", [P, DI, NS])

        xt = m.sb("xt", [P, SU, SEQ + TAPS - 1])
        c_in, c_sig = m.sb("c_in", [P, DI, UC]), m.sb("c_sig", [P, DI, UC])
        z_in, z_sig = m.sb("z_in", [P, DI, UC]), m.sb("z_sig", [P, DI, UC])
        dt_exp, dt_over = m.sb("dt_exp", [P, DI, UC]), m.sb("dt_over", [P, DI, UC])
        b_parts = m.sb("b_parts", [NB, 2, UC], BF16)
        b_rest = m.sb("b_rest", [NB, UC])
        b_mid = m.sb("b_mid", [NB, UC], BF16)
        xc = m.sb("xc", [P, 2, DI, UC])
        z_gate = m.sb("z_gate", [P, 2, DI, UC])
        delta = m.sb("delta", [P, 2, DI, UC])
        dx = m.sb("dx", [P, 2, DI, UC])
        decay = m.sb("decay", [P, ND, GS, SU, SEQ])
        states = m.sb("states", [P, NSC, GS, UC])
        b_all = m.sb("b_all", [P, NBS, GS, UC])
        y_sum = m.sb("y_sum", [P, DI, UC])
        y_gated = m.sb("y_gated", [P, DI, UC])

        zeros_ready = m.sem("zeros_ready")
        a_exp_ready = m.sem("a_exp_ready")
        a_ready = m.sem("a_ready")
        b_lim_ready = m.sem("b_lim_ready")
        w_tap_ready = m.sem("w_tap_ready")
        decay_ready, driven, scanned, read_out, reduced = (
            m.sem(n) for n in ("decay_ready", "driven", "scanned", "read_out", "reduced"))
        br_ready, b_all_ready = m.sem("br_ready"), m.sem("b_all_ready")
        (xt_ready, c0_ready, c1_ready, c0_copied, c1_copied, c_exp, c_lim, c_ln, c_sig_ready, xc_ready,
         bm_ready, b_hi_ready, b_rest_ready, b_mid_ready, b_parts_ready,
         dt0_ready, dt1_ready, dt0_taken, dt1_taken, dt_lim, dt_ln, delta_ready, dx_ready,
         z0_ready, z1_ready, z0_copied, z1_copied, z_exp, z_lim, z_ln, z_sig_ready, gate_ready,
         y_taken, y_ready, out_ready, x_ready) = (m.sem(n) for n in (
             "xt_ready", "c0_ready", "c1_ready", "c0_copied", "c1_copied", "c_exp", "c_lim", "c_ln",
             "c_sig_ready", "xc_ready", "bm_ready", "b_hi_ready", "b_rest_ready", "b_mid_ready",
             "b_parts_ready", "dt0_ready", "dt1_ready", "dt0_taken", "dt1_taken", "dt_lim", "dt_ln",
             "delta_ready", "dx_ready", "z0_ready", "z1_ready", "z0_copied", "z1_copied", "z_exp", "z_lim",
             "z_ln", "z_sig_ready", "gate_ready", "y_taken", "y_ready", "out_ready", "x_ready"))
        block = ctx.enter_context(nc.Block())

        @block.gpsimd
        def _(pool):
            nc.gpsimd.memset(xt[:, :, 0:TAPS - 1], 0.0)
            nc.gpsimd.memset(decay[:, :, :, :, 0:1], 0.0).then_inc(zeros_ready, 1)
            pool.wait_ge(zeros_ready, 1)
            front.gpsimd_rstd(pool, 0)
            front.gpsimd_rstd(pool, 1)

            def take_gate(u, par):
                pool.wait_ge(z_sig_ready, u + 1)
                after(pool, y_ready, u - 1)
                nc.gpsimd.tensor_tensor(z_gate[:, par], z_in[:], z_sig[:], ALU.mult).then_inc(gate_ready, 1)

            def gate_y(u, par):
                pool.wait_ge(y_taken, u + 1)
                after(pool, out_ready, u)
                pool.wait_ge(gate_ready, u + 1)
                nc.gpsimd.tensor_tensor(y_gated[:], y_sum[:], z_gate[:, par], ALU.mult).then_inc(y_ready, 1)

            take_gate(0, 0)

            def body(u, par, first, last):
                for k in range(NI):
                    g, slot = k // 2, k % NSC
                    pool.wait_ge(b_all_ready, u * NG + g + 1)
                    pool.wait_ge(scanned, u * NI + k + 1)
                    nc.gpsimd.tensor_tensor(states[:, slot, :, :], states[:, slot, :, :], b_all[:, g % NBS, :, :],
                                            ALU.mult).then_inc(read_out, 1)
                    if k == 1 and is_unit(u + 2):
                        front.gpsimd_rstd(pool, u + 2)
                    if k == 8 and not first:
                        gate_y(u - 1, 1 - par)
                    if k == 14 and not last:
                        take_gate(u + 1, 1 - par)

            over_units(pool, body)
            gate_y(NU - 1, 1)

        @block.vector
        def _(dve):
            front.vector_stats(dve, 0)
            front.vector_stats(dve, 1)
            weights.await_on(dve)
            nc.vector.tensor_scalar(b_dt_lim[:], b_dt[:], LN_LIM, None, ALU.subtract).then_inc(b_lim_ready, 1)
            for t in range(TAPS):
                op = nc.vector.tensor_tensor(w_tap[:, t, :], w_in[:, 0:DI * P], conv_w[:, t, :], ALU.mult)
            op.then_inc(w_tap_ready, 1)

            def limit(buffer, ready, limited, u, bound):
                dve.wait_ge(ready, u + 1)
                nc.vector.tensor_scalar(buffer[:], buffer[:], bound, None, ALU.min).then_inc(limited, 1)

            def take_xc(u, par):
                dve.wait_ge(c_sig_ready, u + 1)
                nc.vector.tensor_tensor(xc[:, par], c_in[:], c_sig[:], ALU.mult).then_inc(xc_ready, 1)

            def take_b_rest(u, par):
                dve.wait_ge(b_hi_ready, u + 1)
                nc.vector.tensor_tensor(b_rest[:], bank_a[0:NB, :], b_parts[:, par, :],
                                        ALU.subtract).then_inc(b_rest_ready, 1)

            def take_b_low(u, par):
                dve.wait_ge(b_mid_ready, u + 1)
                nc.vector.tensor_tensor(b_parts[BROWS[2]:NB, par, :], b_rest[BROWS[2]:NB, :],
                                        b_mid[BROWS[2]:NB, :], ALU.subtract).then_inc(b_parts_ready, 1)

            def take_delta(u, par):
                dve.wait_ge(dt_ln, u + 1)
                nc.vector.tensor_tensor(delta[:, par], dt_exp[:], dt_over[:], ALU.add).then_inc(delta_ready, 1)
                dve.wait_ge(delta_ready, u + 1)
                nc.vector.tensor_tensor(dx[:, par], delta[:, par], xc[:, par], ALU.mult).then_inc(dx_ready, 1)

            def drive(u, par, k):
                g, h, slot = k // 2, k % 2, k % NSC
                dve.wait_ge(b_all_ready, u * NG + g + 1)
                after(dve, reduced, u * NI + k - NSC + 1)
                if k == 0:
                    dve.wait_ge(dx_ready, u + 1)
                nc.vector.tensor_tensor(states[:, slot, :, :],
                                        dx[:, par, h, :].unsqueeze(1).broadcast_to([P, GS, UC]),
                                        ps_br[:, g % NBR, :, :], ALU.mult).then_inc(driven, 1)

            def scan(u, k):
                slot = k % NSC
                dve.wait_ge(decay_ready, u * NI + k + 1)
                dve.wait_ge(driven, u * NI + k + 1)
                flat = states[:, slot, :, :].rearrange("p n c -> p (n c)")
                nc.vector.tensor_tensor_scan(flat, decay[:, k % ND].rearrange("p n s t -> p (n s t)"), flat,
                                             0.0, ALU.mult, ALU.add).then_inc(scanned, 1)

            def take_y(u, par):
                dve.wait_ge(reduced, (u + 1) * NI)
                after(dve, y_ready, u)
                for h in range(DI):
                    op = nc.vector.scalar_tensor_tensor(y_sum[:, h, :], xc[:, par, h, :], d_skip[:, h:h + 1],
                                                        ps_y[:, h, :], ALU.mult, ALU.add)
                op.then_inc(y_taken, 1)

            def add_out(u):
                dve.wait_ge(out_ready, u + 1)
                nc.vector.tensor_tensor(unit_cols(x_res, u), bank_b[:], unit_cols(x_res, u),
                                        ALU.add).then_inc(x_ready, 1)

            limit(c_sig, c_exp, c_lim, 0, LIM_SIG)
            take_xc(0, 0)
            take_b_rest(0, 0)
            take_b_low(0, 0)
            limit(dt_exp, dt1_taken, dt_lim, 0, LIM_EXP)
            take_delta(0, 0)
            drive(0, 0, 0)
            limit(z_sig, z_exp, z_lim, 0, LIM_SIG)

            def body(u, par, first, last):
                for k in range(NI):
                    if k == 4 and not first:
                        take_y(u - 1, 1 - par)
                    if k + 1 < NI:
                        drive(u, par, k + 1)
                    elif not last:
                        drive(u + 1, 1 - par, 0)
                    scan(u, k)
                    if k == 0 and is_unit(u + 2):
                        front.vector_stats(dve, u + 2)
                    if k == 3 and not last:
                        limit(c_sig, c_exp, c_lim, u + 1, LIM_SIG)
                    if k == 5 and not last:
                        take_xc(u + 1, 1 - par)
                    if k == 8 and not last:
                        take_b_rest(u + 1, 1 - par)
                    if k == 10 and not last:
                        take_b_low(u + 1, 1 - par)
                    if k == 11 and not last:
                        limit(dt_exp, dt1_taken, dt_lim, u + 1, LIM_EXP)
                    if k == 13 and not first:
                        add_out(u - 1)
                    if k == 13 and not last:
                        take_delta(u + 1, 1 - par)
                    if k == 12 and not last:
                        limit(z_sig, z_exp, z_lim, u + 1, LIM_SIG)

            over_units(dve, body)
            take_y(NU - 1, 1)
            add_out(NU - 1)

        @block.tensor
        def _(pe):
            def mm(out, lhsT, rhs, start, stop):
                return nc.tensor.matmul(out, lhsT, rhs, start=start, stop=stop)

            def transpose(u):
                after(pe, dt1_taken, u)
                front.tensor_transpose(pe, u)

            def conv(u, h):
                bank, sem = ((bank_b, c0_ready), (bank_a, c1_ready))[h]
                pe.wait_ge(xt_ready, u + 1)
                if h == 0:
                    after(pe, dt0_taken, u)
                    after(pe, x_ready, u - 2)
                for t in range(TAPS):
                    op = mm(seqs(bank[:]), w_tap[:, t, h * P:(h + 1) * P], xt[:, :, t:t + SEQ],
                            t == 0, t == TAPS - 1)
                op.then_inc(sem, 1)

            def b_matrix(u, par):
                pe.wait_ge(xc_ready, u + 1)
                pe.wait_ge(z0_copied, u + 1)
                for h in range(DI):
                    op = mm(bank_a[0:NB, :], w_b[:, h, :], xc[:, par, h, :], h == 0, h == DI - 1)
                op.then_inc(bm_ready, 1)

            def dt_matrix(u, par, h):
                bank, sem = ((bank_b, dt0_ready), (bank_a, dt1_ready))[h]
                if h == 0:
                    pe.wait_ge(z1_copied, u + 1)
                else:
                    pe.wait_ge(b_rest_ready, u + 1)
                for i in range(DI):
                    op = mm(bank[:], w_dt[:, i, h * P:(h + 1) * P], xc[:, par, i, :], i == 0, i == DI - 1)
                op.then_inc(sem, 1)

            def z_matrix(u, h):
                bank, sem = ((bank_a, z0_ready), (bank_b, z1_ready))[h]
                pe.wait_ge((c1_copied, c0_copied)[h], u + 1)
                mm(seqs(bank[:]), w_in[:, (DI + h) * P:(DI + h + 1) * P], xt[:, :, TAPS - 1:TAPS - 1 + SEQ],
                   True, True).then_inc(sem, 1)

            def replicate(u, par, g):
                if g == 0:
                    pe.wait_ge(b_parts_ready, u + 1)
                after(pe, driven, (u * NG + g - NBR + 1) * 2)
                after(pe, b_all_ready, u * NG + g - NBR + 1)
                for j in range(GS):
                    op = mm(ps_br[:, g % NBR, j, :], consts["select"][:, g * GS + j, :], b_parts[:, par, :], True, True)
                op.then_inc(br_ready, 1)

            def reduce(u, k):
                g, h, slot = k // 2, k % 2, k % NSC
                if k == 0:
                    after(pe, y_taken, u)
                pe.wait_ge(read_out, u * NI + k + 1)
                for j in range(GS):
                    n = g * GS + j
                    op = mm(ps_y[:, h, :], consts["ident"][:], states[:, slot, j, :], n == 0, n == NS - 1)
                op.then_inc(reduced, 1)

            def project_out(u, last):
                pe.wait_ge(y_ready, u + 1)
                pe.wait_ge(dt0_taken, NU if last else u + 3)
                for j in range(TU):
                    for h in range(DI):
                        op = mm(bank_b[:, j * P:(j + 1) * P], y_gated[:, h, j * P:(j + 1) * P], w_out[:, h, :],
                                h == 0, h == DI - 1)
                op.then_inc(out_ready, 1)

            transpose(0)
            pe.wait_ge(w_tap_ready, 1)
            weights.await_on(pe)
            conv(0, 0)
            conv(0, 1)
            z_matrix(0, 0)
            z_matrix(0, 1)
            pe.wait_ge(z0_copied, 1)
            front.tensor_transpose(pe, 1)
            pe.wait_ge(xt_ready, 2)
            b_matrix(0, 0)
            dt_matrix(0, 0, 0)
            dt_matrix(0, 0, 1)
            replicate(0, 0, 0)
            conv(1, 0)
            pe.wait_ge(dt1_taken, 1)
            conv(1, 1)
            LAG = 4

            def body(u, par, first, last):
                for k in range(NI):
                    if k % 2 == 0:
                        if k < NI - 2:
                            replicate(u, par, k // 2 + 1)
                        elif not last:
                            replicate(u + 1, 1 - par, 0)
                    if k >= LAG:
                        reduce(u, k - LAG)
                    elif not first:
                        reduce(u - 1, NI - LAG + k)
                    if k == 3 and not last:
                        z_matrix(u + 1, 0)
                        z_matrix(u + 1, 1)
                    if k == 6 and not last:
                        b_matrix(u + 1, 1 - par)
                        dt_matrix(u + 1, 1 - par, 0)
                    if k == 9 and not last:
                        dt_matrix(u + 1, 1 - par, 1)
                    if k == 11 and not first:
                        project_out(u - 1, last)
                    if k == 11 and is_unit(u + 2):
                        transpose(u + 2)
                    if k == 14 and is_unit(u + 2):
                        conv(u + 2, 0)
                    if k == 15 and is_unit(u + 2):
                        conv(u + 2, 1)

            over_units(pe, body)
            for k in range(NI - LAG, NI):
                reduce(NU - 1, k)
            pe.wait_ge(x_ready, NU - 1)
            project_out(NU - 1, True)

        @block.scalar
        def _(act):
            act.add_instruction(mybir.InstLoadActFuncSet(act_func_set_id=EXP_LN_SET,
                                                         name=nc.get_next_instruction_name()))
            weights.await_on(act)
            nc.scalar.activation(a_exp[:], a_log[:], ACT.Exp).then_inc(a_exp_ready, 1)
            act.wait_ge(a_exp_ready, 1)
            nc.scalar.mul(a_neg[:], a_exp[:], -1.0).then_inc(a_ready, 1)
            act.wait_ge(a_ready, 1)
            act.wait_ge(zeros_ready, 1)
            act.wait_ge(b_lim_ready, 1)

            def copy_xt(u):
                act.wait_ge(front.xn_transposed, u + 1)
                after(act, z1_ready, u)
                nc.scalar.copy(xt[:, :, TAPS - 1:], seqs(bank_a[:])).then_inc(xt_ready, 1)

            def copy_c(u, h):
                bank, ready, copied = ((bank_b, c0_ready, c0_copied), (bank_a, c1_ready, c1_copied))[h]
                after(act, xc_ready, u)
                act.wait_ge(ready, u + 1)
                nc.scalar.activation(c_in[:, h, :], bank[:], ACT.Identity,
                                     bias=conv_b[:, h:h + 1]).then_inc(copied, 1)

            def exp_c(u):
                act.wait_ge(c0_copied, u + 1)
                act.wait_ge(c1_copied, u + 1)
                nc.scalar.activation(c_sig[:], c_in[:], ACT.Exp, scale=-1.0).then_inc(c_exp, 1)

            def sigmoid_c(u):
                act.wait_ge(c_lim, u + 1)
                nc.scalar.activation(c_sig[:], c_sig[:], ACT.Ln, bias=1.0).then_inc(c_ln, 1)
                act.wait_ge(c_ln, u + 1)
                nc.scalar.activation(c_sig[:], c_sig[:], ACT.Exp, scale=-1.0).then_inc(c_sig_ready, 1)

            def first_b_part(u, par):
                act.wait_ge(bm_ready, u + 1)
                after(act, br_ready, (u - 1) * NG)
                nc.scalar.copy(b_parts[:, par, :], bank_a[0:NB, :]).then_inc(b_hi_ready, 1)

            def second_b_part(u, par):
                act.wait_ge(b_rest_ready, u + 1)
                nc.scalar.copy(b_parts[BROWS[1]:BROWS[2], par, :], b_rest[BROWS[1]:BROWS[2], :])
                nc.scalar.copy(b_mid[BROWS[2]:NB, :], b_rest[BROWS[2]:NB, :]).then_inc(b_mid_ready, 1)

            def take_dt(u, h):
                bank, ready, taken = ((bank_b, dt0_ready, dt0_taken), (bank_a, dt1_ready, dt1_taken))[h]
                act.wait_ge(ready, u + 1)
                after(act, delta_ready, u)
                nc.scalar.activation(dt_exp[:, h, :], bank[:], ACT.Exp, bias=b_dt[:, h:h + 1])
                nc.scalar.activation(dt_over[:, h, :], bank[:], ACT.Relu,
                                     bias=b_dt_lim[:, h:h + 1]).then_inc(taken, 1)

            def ln_dt(u):
                act.wait_ge(dt_lim, u + 1)
                nc.scalar.activation(dt_exp[:], dt_exp[:], ACT.Ln, bias=1.0).then_inc(dt_ln, 1)

            def copy_z(u, h):
                bank, ready, copied = ((bank_a, z0_ready, z0_copied), (bank_b, z1_ready, z1_copied))[h]
                after(act, gate_ready, u)
                act.wait_ge(ready, u + 1)
                nc.scalar.copy(z_in[:, h, :], bank[:]).then_inc(copied, 1)

            def exp_z(u):
                act.wait_ge(z0_copied, u + 1)
                act.wait_ge(z1_copied, u + 1)
                nc.scalar.activation(z_sig[:], z_in[:], ACT.Exp, scale=-1.0).then_inc(z_exp, 1)

            def sigmoid_z(u):
                act.wait_ge(z_lim, u + 1)
                nc.scalar.activation(z_sig[:], z_sig[:], ACT.Ln, bias=1.0).then_inc(z_ln, 1)
                act.wait_ge(z_ln, u + 1)
                nc.scalar.activation(z_sig[:], z_sig[:], ACT.Exp, scale=-1.0).then_inc(z_sig_ready, 1)

            def exps(u, par, k):
                g, h = k // 2, k % 2
                after(act, scanned, u * NI + k - ND + 1)
                if k == 0:
                    act.wait_ge(delta_ready, u + 1)
                for j in range(GS):
                    n = g * GS + j
                    op = nc.scalar.activation(decay[:, k % ND, j, :, 1:SEQ], seqs(delta[:, par, h, :])[:, :, 1:SEQ],
                                              ACT.Exp, scale=a_neg[:, h, n:n + 1])
                op.then_inc(decay_ready, 1)

            def copy_b(u, g):
                act.wait_ge(br_ready, u * NG + g + 1)
                after(act, read_out, (u * NG + g - NBS + 1) * 2)
                nc.scalar.copy(b_all[:, g % NBS], ps_br[:, g % NBR]).then_inc(b_all_ready, 1)

            AHEAD = 3
            front.scalar_normalise(act, 0)
            copy_xt(0)
            front.scalar_normalise(act, 1)
            copy_c(0, 0)
            copy_c(0, 1)
            exp_c(0)
            copy_z(0, 0)
            copy_z(0, 1)
            sigmoid_c(0)
            copy_xt(1)
            first_b_part(0, 0)
            take_dt(0, 0)
            second_b_part(0, 0)
            take_dt(0, 1)
            ln_dt(0)
            for k in range(AHEAD):
                exps(0, 0, k)
            copy_b(0, 0)
            exp_z(0)
            sigmoid_z(0)
            copy_c(1, 0)

            def body(u, par, first, last):
                for k in range(NI):
                    if k + AHEAD < NI:
                        exps(u, par, k + AHEAD)
                    elif not last:
                        exps(u + 1, 1 - par, k + AHEAD - NI)
                    if k % 2 == 0:
                        if k < NI - 2:
                            copy_b(u, k // 2 + 1)
                        elif not last:
                            copy_b(u + 1, 0)
                    if k == 6 and is_unit(u + 2):
                        front.scalar_normalise(act, u + 2)
                    if k == 12 and is_unit(u + 2):
                        copy_xt(u + 2)
                    if k == 15 and is_unit(u + 2):
                        copy_c(u + 2, 0)
                    if last:
                        continue
                    if k == 1:
                        copy_c(u + 1, 1)
                    if k == 2:
                        exp_c(u + 1)
                    if k == 4:
                        sigmoid_c(u + 1)
                        copy_z(u + 1, 0)
                        copy_z(u + 1, 1)
                    if k == 7:
                        first_b_part(u + 1, 1 - par)
                    if k == 8:
                        take_dt(u + 1, 0)
                    if k == 9:
                        second_b_part(u + 1, 1 - par)
                        exp_z(u + 1)
                    if k == 10:
                        take_dt(u + 1, 1)
                    if k == 12:
                        ln_dt(u + 1)
                    if k == 12:
                        sigmoid_z(u + 1)

            over_units(act, body)



def start(nc, x_res, consts, att_w, ffn_w, mamba_w, x_head, x_rest, d):
    ident, select, w_b = consts["ident"], consts["select"], mamba_w["w_b"]
    with nc.semaphore("zeroed") as zeroed, nc.semaphore("w_b_zeroed") as w_b_zeroed, nc.Block() as block:
        @block.sync
        def _(sp):
            sp.dma_start(x_res[:, 0:HEAD], d["x"][:, 0:HEAD]).then_inc(x_head, 16)
            att_w.load(sp, att_w["w_qkv"][:], d["W_qkvT"])
            att_w.load(sp, att_w["w_o"][:], d["W_oT"])
            sp.dma_start(x_res[:, HEAD:], d["x"][:, HEAD:]).then_inc(x_rest, 16)
            for name, source in (("wr", "W_rT"), ("wk", "W_kT"), ("wv", "W_vT"), ("mu_r", "mu_r"), ("mu_k", "mu_k")):
                ffn_w.load(sp, ffn_w[name][:], d[source])
            for name, source in (("w_in", "W_in"), ("conv_b", "conv_b"), ("w_dt", "W_dt"), ("b_dt", "b_dt"),
                                 ("a_log", "A_log"), ("d_skip", "Dp"), ("w_out", "W_out")):
                mamba_w.load(sp, mamba_w[name][:], d[source])
            mamba_w.load(sp, mamba_w["conv_w"][:], d["conv_w"].partition_broadcast(P))
            sp.wait_ge(w_b_zeroed, 1)
            for row in BROWS:
                mamba_w.load(sp, w_b[:, :, row:row + NS], d["W_xproj"][:, :, NS:2 * NS])

        @block.gpsimd
        def _(pool):
            nc.gpsimd.memset(w_b[:], 0.0).then_inc(w_b_zeroed, 1)
            for name, value in (("neg_half", -0.5), ("neg_one", -1.0), ("eps", LN_EPS)):
                nc.gpsimd.memset(consts[name][:], value)
            nc.gpsimd.memset(ident[:], 0.0).then_inc(zeroed, 1)
            pool.wait_ge(zeroed, 1)
            nc.gpsimd.affine_select(out=ident[:], in_=ident[:], compare_op=ALU.not_equal, fill=1.0, base=0,
                                    pattern=[[-1, P]], channel_multiplier=1).then_inc(zeroed, 1)
            pool.wait_ge(zeroed, 2)
            nc.gpsimd.memset(select[:], 0.0).then_inc(zeroed, 1)
            pool.wait_ge(zeroed, 3)
            for n, row in enumerate(BROWS):
                nc.gpsimd.affine_select(out=select[:], in_=select[:], compare_op=ALU.not_equal, fill=1.0,
                                        base=-row, pattern=[[-1, NS], [0, P]],
                                        channel_multiplier=1).then_inc(zeroed, 1)
                pool.wait_ge(zeroed, n + 4)


def hybrid_kernel(nc, d):
    with ExitStack() as ctx:
        x_res = ctx.enter_context(nc.sbuf_tensor("x_res", [P, NU, UC], F32))
        consts = {n: ctx.enter_context(nc.sbuf_tensor(n, [P, cols], F32))
                  for n, cols in (("ident", P), ("neg_half", TU), ("neg_one", TU), ("eps", TU))}
        consts["select"] = ctx.enter_context(nc.sbuf_tensor("select", [NB, NS, P], BF16))
        att_w = Weights(nc, ctx, "att", {"w_qkv": [P, 3 * P], "w_o": [P, P]})
        ffn_w = Weights(nc, ctx, "ffn", {"wr": [P, P], "wk": [P, P], "wv": [P, P], "mu_r": [P, 1], "mu_k": [P, 1]})
        mamba_w = Weights(nc, ctx, "mamba", {
            "w_in": [P, 2 * DI * P], "conv_w": [P, TAPS, DI * P], "conv_b": [P, DI], "w_dt": [P, DI, DI * P],
            "b_dt": [P, DI], "a_log": [P, DI, NS], "d_skip": [P, DI], "w_out": [P, DI, P], "w_b": [P, DI, NB]})
        x_head, x_rest = (ctx.enter_context(nc.semaphore(n)) for n in ("x_head", "x_rest"))
        start(nc, x_res, consts, att_w, ffn_w, mamba_w, x_head, x_rest, d)
        if "att" in LAYERS:
            attention_layer(nc, "att", x_res, consts, att_w, x_head, x_rest)
        if "att" not in LAYERS:
            with nc.Block() as block:
                @block.vector
                def _(dve):
                    dve.wait_ge(x_head, 16)
                    dve.wait_ge(x_rest, 16)
        if "ffn1" in LAYERS:
            ffn_layer(nc, "ffn1", x_res, consts, ffn_w, None)
        if "mamba" in LAYERS:
            mamba_layer(nc, "mamba", x_res, consts, mamba_w)
        ffn_layer(nc, "ffn2", x_res, consts, ffn_w, d["out"])


def kernel(**inputs):
    import numpy as np
    import concourse.bacc as bacc
    from concourse.bass_utils import run_bass_kernel_spmd

    def a(name):
        return np.asarray(inputs[name])

    def halves(w):
        return w.reshape(DI, P, -1).transpose(1, 0, 2)

    arrays = {
        "x": a("L0_attn_a_x").reshape(NU, TU, P, P).transpose(2, 0, 1, 3).reshape(P, NU, UC),
        "W_qkvT": np.concatenate([a("L0_attn_a_Wq").T, a("L0_attn_a_Wk").T, a("L0_attn_a_Wv").T], 1),
        "W_oT": a("L0_attn_a_Wo").T,
        "W_in": a("L0_attn_b_W_in"),
        "conv_w": a("L0_attn_b_conv_w")[:, 0, :].T,
        "conv_b": halves(a("L0_attn_b_conv_b"))[:, :, 0],
        "W_xproj": halves(a("L0_attn_b_W_xproj")),
        "W_dt": halves(a("L0_attn_b_W_dt")),
        "b_dt": halves(a("L0_attn_b_b_dt"))[:, :, 0],
        "A_log": halves(a("L0_attn_b_A_log")),
        "Dp": halves(a("L0_attn_b_Dp"))[:, :, 0],
        "W_out": halves(a("L0_attn_b_W_out")),
        "W_rT": a("L0_ffn_W_r").T, "W_kT": a("L0_ffn_W_k").T, "W_vT": a("L0_ffn_W_v").T,
        "mu_r": a("L0_ffn_mu_r").reshape(P, 1), "mu_k": a("L0_ffn_mu_k").reshape(P, 1),
    }
    nc = bacc.Bacc("TRN2", target_bir_lowering=False, num_devices=1)
    dram, feed = {}, {}
    for name, array in arrays.items():
        array = np.ascontiguousarray(array)
        feed[f"in_{name}"] = array
        dram[name] = nc.dram_tensor(f"in_{name}", array.shape, mybir.dt.from_np(array.dtype),
                                    kind="ExternalInput").ap()
    dram["out"] = nc.dram_tensor("out_x", (P, NU, UC), F32, kind="ExternalOutput").ap()
    hybrid_kernel(nc, dram)
    got = run_bass_kernel_spmd(nc, [feed], core_ids=[0]).results[0]["out_x"]
    return got.reshape(P, NU, TU, P).transpose(1, 2, 0, 3).reshape(NSEQ, SEQ, P)
```
